# Optimizing a Trainium2 kernel written in Bass

```python
import numpy as np
import jax
import jax.numpy as jnp

def _softmax(x, axis=-1):
    return jax.nn.softmax(x, axis=axis)

def _gelu(x):
    return jax.nn.gelu(x, approximate=True)

def _silu(x):
    return jax.nn.silu(x)

def _sigmoid(x):
    return jax.nn.sigmoid(x)

def _layernorm(x, axis=-1, eps=1e-05):
    m = jnp.mean(x, axis=axis, keepdims=True)
    v = jnp.var(x, axis=axis, keepdims=True)
    return (x - m) / jnp.sqrt(v + eps)

def _scatter_add(tgt, idx, src, axis=0):
    return tgt.at[idx].add(src)

def _segment_sum(src, seg, n):
    return jax.ops.segment_sum(src, seg, n)
kernel_name = 'mk_gps_d1_gnn_r8_508ab7'

def setup_inputs(seed: int=0):
    np.random.seed(seed)
    _w = jnp.asarray

    def _rec_inputs():
        import jax
        import jax.numpy as jnp
        _gk = jax.random.key(seed)
        x = -0.0003019 + 1 * jax.random.normal(jax.random.fold_in(_gk, 1), (1250, 1024), jnp.float32)
        src = jax.random.randint(jax.random.fold_in(_gk, 2), (20000,), 0, 1250, jnp.int32)
        dst = jnp.minimum((1250 * jax.random.uniform(jax.random.fold_in(_gk, 3), (20000,)) ** 2.0).astype(jnp.int32), 9999)
        _o = jnp.argsort(dst, stable=True)
        src = src[_o]
        dst = dst[_o]
        return (x, src, dst)
    x, src, dst = _rec_inputs()

    def _L0_gnn_setup():
        import jax, jax.numpy as jnp
        import numpy as np
        N = 2500
        E = 40000
        D_IN = 1024
        D_OUT = 1024
        key = jax.random.key(seed)
        k1, k2, k3, k4 = jax.random.split(key, 4)
        x = jax.random.normal(k1, (N, D_IN), dtype=jnp.float32)
        edge_index = jax.random.randint(k2, (2, E), 0, N, dtype=jnp.int64)
        W = jax.random.normal(k3, (D_OUT, D_IN), dtype=jnp.float32) * (1.0 / np.sqrt(D_IN))
        b = jax.random.normal(k4, (D_OUT,), dtype=jnp.float32) * 0.01
        return {'x': x, 'edge_index': edge_index, 'W': W, 'b': b}
    _L0_gnn_all = _L0_gnn_setup()
    _L0_gnn_in = {k: v for k, v in _L0_gnn_all.items() if k in ('W', 'b')}
    del _L0_gnn_all

    def _L0_mix_setup():
        import jax, jax.numpy as jnp
        import numpy as np
        import math
        H = 16
        EPS = 1e-06

        def _apply_kernel(x, orf):
            m, d_k = orf.shape
            proj = jnp.einsum('bhld,md->bhlm', x, orf) / d_k ** 0.25
            norm = jnp.sum(x * x, axis=-1, keepdims=True) / (2.0 * math.sqrt(d_k))
            return (jnp.exp(proj - norm) + EPS) / math.sqrt(m)
        key = jax.random.key(seed)
        ks = jax.random.split(key, 10)
        B, L, D, m = (4, 512, 1024, 256)
        d_k = D // H
        s = 1.0 / math.sqrt(D)
        return {'x': jax.random.normal(ks[0], (B, L, D), jnp.float32), 'Wq': jax.random.normal(ks[1], (D, D), jnp.float32) * s, 'bq': jax.random.normal(ks[2], (D,), jnp.float32) * s, 'Wk': jax.random.normal(ks[3], (D, D), jnp.float32) * s, 'bk': jax.random.normal(ks[4], (D,), jnp.float32) * s, 'Wv': jax.random.normal(ks[5], (D, D), jnp.float32) * s, 'bv': jax.random.normal(ks[6], (D,), jnp.float32) * s, 'Wo': jax.random.normal(ks[7], (D, D), jnp.float32) * s, 'bo': jax.random.normal(ks[8], (D,), jnp.float32) * s, 'orf': jax.random.normal(ks[9], (m, d_k), jnp.float32)}
    _L0_mix_all = _L0_mix_setup()
    _L0_mix_in = {k: v for k, v in _L0_mix_all.items() if k in ('Wq', 'bq', 'Wk', 'bk', 'Wv', 'bv', 'Wo', 'bo', 'orf')}
    del _L0_mix_all

    def _L0_ffn_setup():
        import jax, jax.numpy as jnp
        import numpy as np
        B, S, D, O, E, K = (4, 256, 1024, 1024, 8, 2)
        key = jax.random.key(seed)
        ks = jax.random.split(key, 5)
        scale_in = 1.0 / np.sqrt(D)
        x = jax.random.normal(ks[0], (B, S, D), dtype=jnp.float32)
        gate_w = jax.random.uniform(ks[1], (E, D), jnp.float32, -scale_in, scale_in)
        gate_b = jax.random.uniform(ks[2], (E,), jnp.float32, -scale_in, scale_in)
        expert_w = jax.random.uniform(ks[3], (E, D, O), jnp.float32, -scale_in, scale_in)
        expert_b = jax.random.uniform(ks[4], (E, O), jnp.float32, -scale_in, scale_in)
        return {'x': x, 'gate_w': gate_w, 'gate_b': gate_b, 'expert_w': expert_w, 'expert_b': expert_b}
    _L0_ffn_all = _L0_ffn_setup()
    _L0_ffn_in = {k: v for k, v in _L0_ffn_all.items() if k in ('gate_w', 'gate_b', 'expert_w', 'expert_b')}
    del _L0_ffn_all
    return {'x': x, 'src': src, 'dst': dst, 'L0_gnn_W': _L0_gnn_in['W'], 'L0_gnn_b': _L0_gnn_in['b'], 'L0_mix_Wq': _L0_mix_in['Wq'], 'L0_mix_bq': _L0_mix_in['bq'], 'L0_mix_Wk': _L0_mix_in['Wk'], 'L0_mix_bk': _L0_mix_in['bk'], 'L0_mix_Wv': _L0_mix_in['Wv'], 'L0_mix_bv': _L0_mix_in['bv'], 'L0_mix_Wo': _L0_mix_in['Wo'], 'L0_mix_bo': _L0_mix_in['bo'], 'L0_mix_orf': _L0_mix_in['orf'], 'L0_ffn_gate_w': _L0_ffn_in['gate_w'], 'L0_ffn_gate_b': _L0_ffn_in['gate_b'], 'L0_ffn_expert_w': _L0_ffn_in['expert_w'], 'L0_ffn_expert_b': _L0_ffn_in['expert_b']}

def reference(x, src, dst, L0_gnn_W, L0_gnn_b, L0_mix_Wq, L0_mix_bq, L0_mix_Wk, L0_mix_bk, L0_mix_Wv, L0_mix_bv, L0_mix_Wo, L0_mix_bo, L0_mix_orf, L0_ffn_gate_w, L0_ffn_gate_b, L0_ffn_expert_w, L0_ffn_expert_b):
    import jax
    import jax.numpy as jnp

    def _L0_gnn_ref(x, edge_index, W, b):
        import jax, jax.numpy as jnp
        import numpy as np
        N = 2500
        E = 40000
        D_IN = 1024
        D_OUT = 1024
        num_nodes = x.shape[0]
        self_idx = jnp.arange(num_nodes, dtype=edge_index.dtype)
        ei = jnp.concatenate([edge_index, jnp.stack([self_idx, self_idx], axis=0)], axis=1)
        row, col = (ei[0], ei[1])
        h = jnp.einsum('nd,od->no', x, W) + b
        deg = jnp.zeros((num_nodes,), dtype=h.dtype).at[row].add(1.0)
        deg_inv_sqrt = deg ** (-0.5)
        norm = deg_inv_sqrt[row] * deg_inv_sqrt[col]
        msg = norm[:, None] * h[col]
        out = jax.ops.segment_sum(msg, row, num_segments=num_nodes)
        return out

    def _L0_mix_ref(x, Wq, bq, Wk, bk, Wv, bv, Wo, bo, orf):
        import jax, jax.numpy as jnp
        import numpy as np
        import math
        H = 16
        EPS = 1e-06

        def _apply_kernel(x, orf):
            m, d_k = orf.shape
            proj = jnp.einsum('bhld,md->bhlm', x, orf) / d_k ** 0.25
            norm = jnp.sum(x * x, axis=-1, keepdims=True) / (2.0 * math.sqrt(d_k))
            return (jnp.exp(proj - norm) + EPS) / math.sqrt(m)
        B, L, D = x.shape
        d_k = D // H

        def split(y):
            return y.reshape(B, L, H, d_k).transpose(0, 2, 1, 3)
        q = split(x @ Wq.T + bq)
        k = split(x @ Wk.T + bk)
        v = split(x @ Wv.T + bv)
        q_phi = _apply_kernel(q, orf)
        k_phi = _apply_kernel(k, orf)
        kv = jnp.einsum('bhlm,bhld->bhmd', k_phi, v)
        ksum = jnp.sum(k_phi, axis=2)
        num = jnp.einsum('bhlm,bhmd->bhld', q_phi, kv)
        den = jnp.einsum('bhlm,bhm->bhl', q_phi, ksum)
        out = num / den[..., None]
        out = out.transpose(0, 2, 1, 3).reshape(B, L, D)
        return out @ Wo.T + bo

    def _L0_ffn_ref(x, gate_w, gate_b, expert_w, expert_b):
        import jax, jax.numpy as jnp
        import numpy as np
        B, S, D, O, E, K = (4, 256, 1024, 1024, 8, 2)
        logits = jnp.einsum('bsd,ed->bse', x, gate_w) + gate_b
        if K < E:
            topv, topi = jax.lax.top_k(logits, K)
            keep = jax.nn.one_hot(topi, E, dtype=jnp.float32).sum(axis=-2)
            logits = jnp.where(keep > 0, logits, -jnp.inf)
        gate_score = jax.nn.softmax(logits, axis=-1)
        expert_out = jnp.einsum('bsd,edo->bseo', x, expert_w) + expert_b
        out = jnp.einsum('bseo,bse->bso', expert_out, gate_score)
        return out
    edge_index = jnp.stack([src, dst])
    xn = _layernorm(x, axis=-1)
    x = x + _L0_gnn_ref(xn, edge_index, L0_gnn_W, L0_gnn_b) + _L0_mix_ref(xn[None], L0_mix_Wq, L0_mix_bq, L0_mix_Wk, L0_mix_bk, L0_mix_Wv, L0_mix_bv, L0_mix_Wo, L0_mix_bo, L0_mix_orf)[0]
    x = x + _L0_ffn_ref(_layernorm(x, axis=-1)[None], L0_ffn_gate_w, L0_ffn_gate_b, L0_ffn_expert_w, L0_ffn_expert_b)[0]
    return x

_drawn_inputs = setup_inputs


def setup_inputs(seed=0):
    import zlib

    import numpy as np

    out = dict(_drawn_inputs(seed))
    spreads = {}
    factors = {'L0_ffn_expert_b': 4.92}
    for name, (base, spread) in spreads.items():
        noise = np.random.default_rng([zlib.crc32(name.encode()), seed]).standard_normal(out[name].shape)
        drawn = base * np.exp(spread * noise) if base else spread * noise
        out[name] = jnp.asarray(drawn.astype(out[name].dtype))
    for name, factor in factors.items():
        out[name] = (out[name] * factor).astype(out[name].dtype)
    return out
```

```python
from contextlib import ExitStack

import concourse.bass as bass
from concourse import mybir

P = 128
N, D = 1250, 1024
TT = -(-N // P)
NP = TT * P
LAST = N - (TT - 1) * P
KT = D // P
CW = 512
NC = D // CW
H, DK, M = 16, 64, 256
MH = M // P
E = 8
EDGES = 20000
PAIR = 2 * P
PAIRS = -(-EDGES // PAIR) + 1
CHUNKS = ((0, 512), (512, 512), (1024, NP - 1024))
EPS_LN = 1e-5
EPS_PHI = 1e-6
START = 1
PHI_SCALE = float(DK) ** -0.25
SQ_SCALE = (1.0 / (2.0 * DK ** 0.5) / PHI_SCALE) ** 0.5

ALU = mybir.AluOpType
ACT = mybir.ActivationFunctionType
AX = mybir.AxisListType
F32 = mybir.dt.float32
F32R = mybir.dt.float32r
BF16 = mybir.dt.bfloat16
F16 = mybir.dt.float16
I32 = mybir.dt.int32
U32 = mybir.dt.uint32
ds = bass.ds
RMAX = bass.bass_isa.ReduceOp.max


def gps_layer(nc, x, dst_pairs, src_cols, dst_cols, wg, bg, wq, bq, wk, bk, wv, bv, wo, bo, orf,
              gate_w, gate_b, expert_w, expert_b, out):
    y1 = nc.dram_tensor("y1_scratch", [NC, TT, P, CW], F32, kind="Internal").ap()
    ctx = ExitStack()
    with ctx:
        def sem(name):
            return ctx.enter_context(nc.semaphore(name))

        def keep(name, shape, dt, where=ctx):
            return where.enter_context(nc.sbuf_tensor(name, shape, dt))

        ident = keep("ident", [P, P], F32)
        ones = keep("ones", [P, P], F32)
        dis = keep("dis", [P, TT], F32)
        adis = keep("adis", [P, TT], F32)
        sums = keep("sums", [P, TT], F32)
        negmean = keep("negmean", [P, TT], F32)
        ssq = keep("ssq", [P, TT], F32)
        varx = keep("varx", [P, TT], F32)
        rstd = keep("rstd", [P, TT], F32)
        mhalf = keep("mhalf", [P, TT], F32)
        deg = keep("deg", [P, TT], F32)
        biasT = keep("biasT", [P, 3, KT], F32)
        PB = ctx.enter_context(nc.psum_tensor("PB", [P, 8 * 512], F32))

        s0 = ExitStack()
        xn = keep("xn", [P, TT, D], F32, s0)
        s0.close()
        s0 = ExitStack()
        attnT = keep("attnT", [P, KT, NP], F32, s0)
        s0.close()
        x2nT = keep("x2nT", [P, KT, NP], F32)

        pa = ExitStack()
        xh = keep("xh", [P, KT, NP], F32R, pa)
        xl = keep("xl", [P, KT, NP], F32R, pa)
        hw = keep("hw", [P, 3, 2, KT, P], F32R, pa)
        hraw = keep("hraw", [P, KT, P], F32, pa)
        tk = keep("tk", [P, 2, NP], F32R, pa)
        sk = keep("sk", [P, 2, NP], F32R, pa)
        qphi = keep("qphi", [P, MH, NP], F32, pa)
        vT = qphi[:, 0, :]
        kphi = keep("kphi", [P, TT, M], F32, pa)
        att = kphi[:, :, 0:P]
        vt = keep("vt", [P, TT, 2, DK + 1], F32, pa)
        qf = keep("qf", [P, CW], F32, pa)
        sqf = keep("sqf", [P, CW], F32, pa)
        kvs = keep("kvs", [P, 2, MH, DK + 1], F32, pa)
        rec = keep("rec", [P, TT // 2], F32, pa)
        orfh = keep("orfh", [P, M], F32R, pa)
        orfl = keep("orfl", [P, M], F32R, pa)
        negr = keep("negr", [P, M], F32R, pa)
        pa.close()

        s1 = ExitStack()
        axT = keep("axT", [P, KT, NP], F32, s1)
        s1.close()
        x2 = keep("x2", [P, TT, D], F32)

        pg = ExitStack()
        AT = keep("AT", [P, TT, NP], F32, pg)
        xs = keep("xs", [P, 2, TT, P], F32, pg)
        iota = keep("iota", [P, NP], F16, pg)
        diag = keep("diag", [P, 2 * NP - P], BF16, pg)
        ohs = keep("ohs", [P, 4, NP], BF16, pg)
        ohd = keep("ohd", [P, 4, P], BF16, pg)
        degacc = keep("degacc", [P, NP], F32, pg)
        sci = keep("sci", [P, 2 * PAIRS], I32, pg)
        dci = keep("dci", [P, 2 * PAIRS], I32, pg)
        sc = keep("sc", [P, 2 * PAIRS], F32, pg)
        dc = keep("dc", [P, 2 * PAIRS], F32, pg)
        dpi = keep("dpi", [PAIRS, PAIR], I32, pg)
        dpf = keep("dpf", [PAIRS, PAIR], F32, pg)
        dmin = keep("dmin", [PAIRS, 1], F32, pg)
        dmax = keep("dmax", [PAIRS, 1], F32, pg)
        blo = keep("blo", [PAIRS, TT], F32, pg)
        bhi = keep("bhi", [PAIRS, TT], F32, pg)
        up = keep("up", [PAIRS, 1], F32, pg)
        down = keep("down", [PAIRS, 1], F32, pg)
        rel = keep("rel", [PAIRS, TT], F32, pg)
        ext = keep("ext", [PAIRS, 2 * TT], F32, pg)
        extr = keep("extr", [PAIRS, 2 * TT], F32, pg)
        rng = keep("rng", [1, 4, TT], F32, pg)
        rngi = keep("rngi", [1, 4, TT], I32, pg)
        junk = keep("junk", [P, D], F32, pg)
        dscr = keep("dscr", [P, P], F32, pg)
        scaled = keep("scaled", [P, NP], F32, pg)
        pg.close()

        wh = keep("wh", [P, 2, KT, CW], F32R)
        wl = keep("wl", [P, 2, KT, CW], F32R)
        raw = keep("raw", [P, 4, CW], F32)
        sth = keep("sth", [P, 2, KT, P], F32R)
        stl = keep("stl", [P, 2, KT, P], F32R)
        yrow = keep("yrow", [P, 2, CW], F32)
        pr = ExitStack()
        xrow = keep("xrow", [P, 2, CW], F32, pr)
        bgb = keep("bgb", [P, D], F32, pr)
        bob = keep("bob", [P, D], F32, pr)
        u1 = keep("u1", [P, CW], F32, pr)
        u2 = keep("u2", [P, CW], F32, pr)
        pr.close()
        xhat = keep("xhat", [P, 2, D], F32)
        stats = keep("stats", [P, 2, 6], F32)
        aggr = keep("aggr", [P, TT, 2], F32)
        gw = keep("gw", [P, KT, E], F32)
        gb = keep("gb", [E, 1], F32)
        eb = keep("eb", [E, D], F32)
        lgT = keep("lgT", [E, NP], F32)
        lg = keep("lg", [P, TT, E], F32)
        mx = keep("mx", [P, TT, 8], F32)
        ix = keep("ix", [P, TT, 8], U32)
        ixf = keep("ixf", [P, TT, 8], F32)
        gd = keep("gd", [P, 4, TT], F32)
        iota8 = keep("iota8", [P, E], F32)
        gate = keep("gate", [P, TT, E], F32)
        gate2 = keep("gate2", [P, TT, E], F32)
        gateT = keep("gateT", [E, NP], F32)

        def bank(b, n=CW):
            return PB[:, 512 * b:512 * b + n]

        s_edges = [sem(f"s_edges{i}") for i in range(3)]
        s_x = [sem(f"s_x{t}") for t in range(TT)]
        s_bias = [sem(f"s_bias{i}") for i in range(10)]
        s_const = sem("s_const")
        s_apart = {e.engine: sem(f"s_apart{n}") for n, e in enumerate((nc.scalar, nc.gpsimd, nc.tensor))}
        s_cst2 = sem("s_cst2")
        s_dchain = sem("s_dchain")
        s_ext = sem("s_ext")
        s_extr = sem("s_extr")
        s_rng = sem("s_rng")
        oh_ready = sem("oh_ready")
        oh_free = sem("oh_free")
        at_done = sem("at_done")
        at_evac = sem("at_evac")
        ln_a = sem("ln_a")
        s_degacc = sem("s_degacc")
        s_deg = sem("s_deg")
        s_degcol = sem("s_degcol")
        s_dis = sem("s_dis")
        s_rstd = sem("s_rstd")
        s_pchain = sem("s_pchain")
        s_xn = sem("s_xn")
        xs_ready = sem("xs_ready")
        ax_done = sem("ax_done")
        ax_evac = sem("ax_evac")
        s_ad = sem("s_ad")
        s_adcol = sem("s_adcol")

        class Rows:
            def __init__(self, name, chunks):
                self.chunks = chunks
                self.raw = [sem(f"{name}_raw{i}") for i in range(4)]
                self.whigh = sem(f"{name}_whigh")
                self.wready = sem(f"{name}_wready")
                self.high = sem(f"{name}_high")
                self.low = sem(f"{name}_low")
                self.done = sem(f"{name}_done")
                self.free = sem(f"{name}_free")

        rg, ro, rm = Rows("rg", NC), Rows("ro", NC), Rows("rm", E * NC)
        g_x = [sem(f"g_x{i}") for i in range(2)]
        g_c = sem("g_c")
        g_out = [sem(f"g_out{i}") for i in range(2)]
        o_y = [sem(f"o_y{i}") for i in range(2)]
        xt_done = sem("xt_done")
        xt_high = sem("xt_high")
        xt_low = sem("xt_low")
        a_raw = sem("a_raw")
        a_high = sem("a_high")
        a_w = sem("a_w")
        a_orf = sem("a_orf")
        a_cst = sem("a_cst")
        proj_done = sem("proj_done")
        qf_ready = sem("qf_ready")
        sq_ready = sem("sq_ready")
        vt_ready = sem("vt_ready")
        t_hi = sem("t_hi")
        t_done = sem("t_done")
        s_hi = sem("s_hi")
        s_done = sem("s_done")
        phi_done = sem("phi_done")
        exp_done = sem("exp_done")
        kph_ready = sem("kph_ready")
        qph_ready = sem("qph_ready")
        kv_done = sem("kv_done")
        kv_evac = sem("kv_evac")
        aux_done = sem("aux_done")
        aux_evac = sem("aux_evac")
        rec_done = sem("rec_done")
        y_ready = sem("y_ready")
        s_mean = sem("s_mean")
        s_rstd2 = sem("s_rstd2")
        s_xhat = sem("s_xhat")
        x2t_done = sem("x2t_done")
        x2t_evac = sem("x2t_evac")
        lg_done = sem("lg_done")
        lg_evac = sem("lg_evac")
        lgt_done = sem("lgt_done")
        s_gd = sem("s_gd")
        s_ge = sem("s_ge")
        s_gate = sem("s_gate")
        gt_done = sem("gt_done")
        gt_evac = sem("gt_evac")
        eb_done = sem("eb_done")
        eb_evac = sem("eb_evac")
        s_out = sem("s_out")

        block = ctx.enter_context(nc.Block())

        def apart(eng):
            eng.sem_inc(s_apart[eng.engine], 1)

        def graph_over(eng):
            eng.wait_ge(y_ready, START + NC * TT)
            eng.wait_ge(rg.high, NC * TT + 2)
            eng.wait_ge(rg.low, NC * TT + 1)
            for i in range(2):
                eng.wait_ge(g_out[i], START + 16 * NC * TT // 2)

        def attention_over(eng):
            eng.wait_ge(aux_evac, 12 * KT + 2)

        @block.sync
        def _(sp):
            sp.dma_start(dpi[:, :], dst_pairs).then_inc(s_edges[0], 16)
            sp.dma_start(sci[:, :], src_cols).then_inc(s_edges[1], 16)
            sp.dma_start(dci[:, :], dst_cols).then_inc(s_edges[2], 16)
            for t in range(TT):
                sp.dma_start(xn[:, t, :], x[t * P:(t + 1) * P, :]).then_inc(s_x[t], 16)
            for i, b in enumerate((bk, bv, bq)):
                sp.dma_start(biasT[:, i, :], b).then_inc(s_bias[i], 16)

            def load_weights(r, w):
                for i in range(4):
                    sp.dma_start(raw[:, i, :], w[i // KT, i % KT]).then_inc(r.raw[i], 16)
                with sp.Fori(1, r.chunks * KT // 4) as g:
                    for i in range(4):
                        sp.wait_ge(r.wready, 4 * g - 3 + i)
                        s = 4 * g + i
                        sp.dma_start(raw[:, i, :], w.rearrange("c k p n -> (c k) p n")[ds(s, 1)].rearrange("a p n -> (a p) n")).then_inc(r.raw[i], 16)

            sp.wait_ge(ax_done, KT)
            sp.wait_ge(ax_evac, KT + 2)
            sp.wait_ge(s_adcol, TT)
            sp.dma_start(bgb[:, :], bg.broadcast_to([P, D])).then_inc(s_bias[3], 16)
            sp.dma_start(bob[:, :], bo.broadcast_to([P, D])).then_inc(s_bias[4], 16)
            load_weights(rg, wg)
            for c in range(NC):
                def load_x(t, i):
                    sp.dma_start(xrow[:, i, :], x[ds(P * t, P), c * CW:(c + 1) * CW]).then_inc(g_x[i], 16)

                def store_y(t, i):
                    sp.wait_ge(y_ready, START + TT * c + t + 1)
                    sp.dma_start(y1[c, ds(t, 1)].rearrange("a p n -> (a p) n"), yrow[:, i, :]).then_inc(g_out[i], 16)

                for i in range(2):
                    load_x(i, i)
                with sp.Fori(0, TT // 2 - 1) as g:
                    for i in range(2):
                        store_y(2 * g + i, i)
                        load_x(2 * g + 2 + i, i)
                for i in range(2):
                    store_y(TT - 2 + i, i)

            graph_over(sp)
            sp.dma_start(qf[:, 0:M], orf).then_inc(a_orf, 16)
            with sp.Fori(0, KT) as j:
                for i, w in enumerate((wk, wv, wq)):
                    sp.wait_ge(a_w, START + 3 * j + i)
                    sp.dma_start(hraw[:, :, :], w[ds(j, 1)].rearrange("a p k n -> (a p) k n")).then_inc(a_raw, 16)

            attention_over(sp)
            load_weights(ro, wo)
            for c in range(NC):
                for i in range(2):
                    if c:
                        sp.wait_ge(ro.free, TT * c + 1 + i)
                    sp.dma_start(yrow[:, i, :], y1[c, i]).then_inc(o_y[i], 16)
                with sp.Fori(1, TT // 2) as g:
                    for i in range(2):
                        sp.wait_ge(ro.free, TT * c + 2 * g + 1 + i)
                        sp.dma_start(yrow[:, i, :], y1[c, ds(2 * g + i, 1)].rearrange("a p n -> (a p) n")).then_inc(o_y[i], 16)
            sp.dma_start(gw[:, :, :], gate_w).then_inc(s_bias[5], 16)
            sp.dma_start(gb[:, :], gate_b).then_inc(s_bias[6], 16)
            sp.dma_start(eb[:, :], expert_b).then_inc(s_bias[7], 16)
            sp.wait_ge(ro.wready, NC * KT)
            load_weights(rm, expert_w)
            for c in range(NC):
                at = (E - 1) * NC + c
                with sp.Fori(0, TT - 1) as t:
                    sp.wait_ge(rm.free, TT * at + t + 3)
                    sp.dma_start(out[ds(P * t, P), c * CW:(c + 1) * CW],
                                 x2[:, ds(t, 1), c * CW:(c + 1) * CW].rearrange("p a n -> p (a n)")).then_inc(s_out, 16)
                sp.wait_ge(rm.free, TT * at + TT + 2)
                sp.dma_start(out[P * (TT - 1):N, c * CW:(c + 1) * CW],
                             x2[0:LAST, TT - 1, c * CW:(c + 1) * CW]).then_inc(s_out, 16)
            sp.wait_ge(s_out, 16 * NC * TT)

        @block.gpsimd
        def _(pool):
            g = nc.gpsimd
            g.memset(ident[:, :], 0.0).then_inc(s_const, 1)
            g.memset(diag[:, :], 0.0).then_inc(s_const, 1)
            pool.wait_ge(s_const, 2)
            g.affine_select(out=ident[:, :], in_=ident[:, :], compare_op=ALU.not_equal, fill=1.0, base=0,
                            pattern=[[-1, P]], channel_multiplier=1).then_inc(s_cst2, 1)
            g.affine_select(out=diag[:, NP - P:NP], in_=diag[:, NP - P:NP], compare_op=ALU.not_equal, fill=1.0,
                            base=0, pattern=[[-1, P]], channel_multiplier=1).then_inc(s_cst2, 1)
            g.iota(iota[:, :], [[1, NP]], base=0, channel_multiplier=0,
                   allow_small_or_imprecise_dtypes=True).then_inc(s_cst2, 1)
            g.iota(blo[:, :], [[P, TT]], base=0, channel_multiplier=0,
                   allow_small_or_imprecise_dtypes=True).then_inc(s_cst2, 1)
            g.iota(bhi[:, :], [[P, TT]], base=P - 1, channel_multiplier=0,
                   allow_small_or_imprecise_dtypes=True).then_inc(s_cst2, 1)
            g.iota(up[:, :], [[0, 1]], base=1, channel_multiplier=1,
                   allow_small_or_imprecise_dtypes=True).then_inc(s_cst2, 1)
            g.iota(down[:, :], [[0, 1]], base=PAIRS, channel_multiplier=-1,
                   allow_small_or_imprecise_dtypes=True).then_inc(s_cst2, 1)
            g.memset(ones[:, :], 1.0).then_inc(s_cst2, 1)
            g.memset(mhalf[:, :], -0.5).then_inc(s_cst2, 1)
            g.memset(degacc[:, :], 0.0).then_inc(s_pchain, 1)
            pool.sem_inc(oh_free, 4)
            pool.sem_inc(at_evac, 2)
            pool.sem_inc(ax_evac, 2)
            for r in (rg, ro, rm):
                pool.sem_inc(r.free, 2)
            pool.sem_inc(proj_done, 6)
            pool.sem_inc(qf_ready, 3)
            pool.sem_inc(exp_done, 2)
            pool.sem_inc(aux_evac, 2)

            for signal in (a_w, t_done, s_done, sq_ready, phi_done, kv_done, aux_done, kv_evac, g_c, y_ready, *g_out):
                pool.sem_inc(signal, START)

            pool.wait_ge(s_ext, 1)
            g.partition_all_reduce(extr[:, :], ext[:, :], PAIRS, RMAX).then_inc(s_extr, 1)

            with pool.Fori(0, TT) as b:
                pool.wait_ge(at_evac, b + 3)
                pool.wait_ge(s_pchain, b + 1)
                g.tensor_tensor(degacc[:, :], degacc[:, :], AT[:, ds(b, 1), :].rearrange("p a n -> p (a n)"), ALU.add).then_inc(s_pchain, 1)
            pool.wait_ge(s_pchain, TT + 1)
            pool.wait_ge(ln_a, 3 * TT)
            g.tensor_scalar(varx[:, :], ssq[:, :], 1.0 / D, EPS_LN, ALU.mult, ALU.add).then_inc(s_degacc, 1)
            pool.wait_ge(s_degacc, 1)
            g.tensor_tensor(rstd[:, :], varx[:, :], mhalf[:, :], ALU.pow).then_inc(s_rstd, 1)
            pool.wait_ge(s_degcol, TT)
            g.tensor_tensor(dis[:, :], deg[:, :], mhalf[:, :], ALU.pow).then_inc(s_dis, 1)
            pool.wait_ge(s_dis, 1)
            g.memset(degacc[:, :], 0.0).then_inc(s_pchain, 1)
            for t in range(TT):
                pool.wait_ge(s_pchain, TT + 2 + 2 * t)
                g.tensor_scalar(scaled[:, :], AT[:, t, :], dis[:, t:t + 1], None, ALU.mult).then_inc(s_pchain, 1)
                pool.wait_ge(s_pchain, TT + 3 + 2 * t)
                g.tensor_tensor(degacc[:, :], degacc[:, :], scaled[:, :], ALU.add).then_inc(s_pchain, 1)

            def split_weights(r):
                with pool.Fori(0, 2) as c:
                    for k in range(KT):
                        split_slab(r, c, k)
                if r.chunks > 2:
                    with pool.Fori(2, r.chunks) as c:
                        pool.wait_ge(r.done, TT * (c - 1))
                        for k in range(KT):
                            split_slab(r, c, k)

            def split_slab(r, c, k):
                cp = c % 2 if isinstance(c, int) else c & 1
                pool.wait_ge(r.raw[k % 4], 16 * (2 * c + k // 4 + 1))
                g.tensor_copy(wh[:, ds(cp, 1), k, :].rearrange("p a n -> p (a n)"), raw[:, k % 4, :]).then_inc(r.whigh, 1)
                pool.wait_ge(r.whigh, KT * c + k + 1)
                g.tensor_tensor(wl[:, ds(cp, 1), k, :].rearrange("p a n -> p (a n)"), raw[:, k % 4, :],
                                wh[:, ds(cp, 1), k, :].rearrange("p a n -> p (a n)").bitcast(F32), ALU.subtract).then_inc(r.wready, 1)

            pool.wait_ge(ax_done, KT)
            pool.wait_ge(s_adcol, TT)
            split_weights(rg)

            graph_over(pool)
            g.memset(negr[:, :].bitcast(F32), -1.0).then_inc(a_cst, 1)
            g.memset(vt[:, :, :, DK:DK + 1], 1.0).then_inc(a_cst, 1)
            pool.wait_ge(a_orf, 16)
            g.tensor_copy(orfh[:, :], qf[:, 0:M]).then_inc(a_cst, 1)
            pool.wait_ge(a_cst, 3)
            g.tensor_tensor(orfl[:, :], qf[:, 0:M], orfh[:, :].bitcast(F32), ALU.subtract).then_inc(a_cst, 1)

            def split_head(j, i):
                pool.wait_ge(proj_done, 9 * j + 3 * i)
                pool.wait_ge(a_raw, 16 * (3 * j + i + 1))
                apart(pool)
                g.tensor_copy(hw[:, i, 0], hraw[:, :, :]).then_inc(a_high, 1)
                pool.wait_ge(a_high, 3 * j + i + 1)
                g.tensor_tensor(hw[:, i, 1], hraw[:, :, :], hw[:, i, 0].bitcast(F32), ALU.subtract).then_inc(a_w, 1)

            for i in range(3):
                split_head(0, i)

            with pool.Fori(0, KT - 1) as j:
                for i in range(3):
                    split_head(j + 1, i)

            attention_over(pool)
            split_weights(ro)
            g.iota(iota8[:, :], [[1, E]], base=0, channel_multiplier=0,
                   allow_small_or_imprecise_dtypes=True).then_inc(s_gate, 1)
            pool.wait_ge(s_mean, TT)
            g.tensor_scalar(varx[:, :], aggr[:, :, 1:2].rearrange("p t a -> p (t a)"), EPS_LN, None, ALU.add).then_inc(s_rstd2, 1)
            pool.wait_ge(s_rstd2, 1)
            g.tensor_tensor(rstd[:, :], varx[:, :], mhalf[:, :], ALU.pow).then_inc(s_rstd2, 1)
            pool.wait_ge(ro.done, NC * TT)
            split_weights(rm)

        @block.scalar
        def _(act):
            a = nc.scalar
            for b in range(TT):
                act.wait_ge(s_x[b], 16)
                act.wait_ge(ln_a, 3 * b)
                a.activation(junk[:, :], xn[:, b, :], ACT.Identity, accum_out=sums[:, b:b + 1]).then_inc(ln_a, 1)
                act.wait_ge(ln_a, 3 * b + 1)
                a.mul(negmean[:, b:b + 1], sums[:, b:b + 1], -1.0 / D).then_inc(ln_a, 1)
                act.wait_ge(ln_a, 3 * b + 2)
                a.activation(junk[:, :], xn[:, b, :], ACT.Square, bias=negmean[:, b:b + 1],
                             accum_out=ssq[:, b:b + 1]).then_inc(ln_a, 1)
                act.wait_ge(at_done, b + 1)
                s = 1536 * (b % 2)
                a.activation(AT[:, b, :], PB[:, s:s + NP], ACT.Copy).then_inc(at_evac, 1)

            with act.Fori(0, KT // 2) as j2:
                for p in range(2):
                    j = 2 * j2
                    act.wait_ge(ax_done, j + p + 1)
                    a.activation(axT[:, ds(j + p, 1), :].rearrange("p a n -> p (a n)"), PB[:, 1536 * p:1536 * p + NP],
                                 ACT.Copy).then_inc(ax_evac, 1)

            def highs(r, src):
                for p in range(2):
                    a.activation(sth[:, p], src[:, :, p * P:(p + 1) * P], ACT.Copy).then_inc(r.high, 1)
                with act.Fori(0, r.chunks) as c:
                    with act.Fori(0, TT // 2 - 1) as g:
                        for p in range(2):
                            act.wait_ge(r.done, TT * c + 2 * g + p + 1)
                            a.activation(sth[:, p], src[:, :, ds(P * (2 * g + 2 + p), P)], ACT.Copy).then_inc(r.high, 1)
                    for p in range(2):
                        act.wait_ge(r.done, TT * c + TT - 1 + p)
                        a.activation(sth[:, p], src[:, :, p * P:(p + 1) * P], ACT.Copy).then_inc(r.high, 1)

            act.wait_ge(ax_evac, KT + 2)
            act.wait_ge(s_adcol, TT)
            highs(rg, axT)

            for i in range(2 * TT):
                t, k0 = i // 2, 4 * (i % 2)
                act.wait_ge(xt_done, i + 1)
                if i == 0:
                    graph_over(act)
                a.activation(xh[:, k0:k0 + 4, t * P:(t + 1) * P],
                             bank(i % 4).rearrange("p (k n) -> p k n", k=4), ACT.Copy).then_inc(xt_high, 1)

            act.wait_ge(a_cst, 4)
            act.wait_ge(s_bias[0], 16)
            act.wait_ge(s_bias[1], 16)
            act.wait_ge(s_bias[2], 16)
            act.wait_ge(xt_low, 2 * TT)

            def project(j, i, wi):
                c0, n = CHUNKS[i % 3]
                act.wait_ge(proj_done, 6 + 9 * j + 3 * wi + i % 3 + 1)
                act.wait_ge(t_done, START + 6 * j + i)
                act.wait_ge(sq_ready, START + 6 * j + i)
                act.wait_ge(s_done, START + 6 * j + i)
                apart(act)
                a.activation(qf[:, 0:n], bank(i % 3, n), ACT.Identity,
                             bias=biasT[:, wi, ds(j, 1)]).then_inc(qf_ready, 1)
                act.wait_ge(qf_ready, 3 + 6 * j + i + 1)
                a.activation(sqf[:, 0:n], qf[:, 0:n], ACT.Square, scale=SQ_SCALE).then_inc(sq_ready, 1)
                act.wait_ge(sq_ready, START + 6 * j + i + 1)
                act.wait_ge(phi_done, START + 22 * j + (10 if i >= 3 else 0))
                a.activation(sk[0:64, 0, c0:c0 + n], sqf[0:64, 0:n], ACT.Copy)
                a.activation(sk[64:128, 1, c0:c0 + n], sqf[64:128, 0:n], ACT.Copy).then_inc(s_hi, 1)

            with act.Fori(0, KT) as j:
                for i in range(3):
                    project(j, i, 0)
                act.wait_ge(aux_done, START + 12 * j)
                for i in range(3):
                    c0, n = CHUNKS[i]
                    act.wait_ge(proj_done, 6 + 9 * j + 3 + i + 1)
                    apart(act)
                    a.activation(vT[:, c0:c0 + n], bank(i, n), ACT.Identity,
                                 bias=biasT[:, 1, ds(j, 1)]).then_inc(vt_ready, 1)
                for h in range(2):
                    act.wait_ge(kv_done, START + 2 * j + h)
                    act.wait_ge(aux_done, START + 12 * j)
                    for i in range(TT // 2):
                        f = 5 * h + i
                        act.wait_ge(phi_done, START + 22 * j + f + 1)
                        a.activation(kphi[:, 2 * i:2 * i + 2, :], bank(3 + f % 2).rearrange("p (t m) -> p t m", t=2),
                                     ACT.Exp, scale=PHI_SCALE).then_inc(exp_done, 1)
                for i in range(3, 6):
                    project(j, i, 2)
                for h in range(2):
                    act.wait_ge(aux_done, START + 12 * j + 4 + 2 * h)
                    for i in range(6):
                        f = 10 + 6 * h + i
                        c0, n = CHUNKS[i // 2]
                        act.wait_ge(phi_done, START + 22 * j + f + 1)
                        a.activation(qphi[:, i % 2, c0:c0 + n], bank(3 + f % 2, n), ACT.Exp,
                                     scale=PHI_SCALE).then_inc(exp_done, 1)

            attention_over(act)
            highs(ro, attnT)

            for i in range(2 * TT):
                t, k0 = i // 2, 4 * (i % 2)
                act.wait_ge(x2t_done, i + 1)
                if i == 0:
                    act.wait_ge(ro.low, NC * TT + 1)
                    act.wait_ge(ro.high, NC * TT + 2)
                a.activation(x2nT[:, k0:k0 + 4, t * P:(t + 1) * P],
                             bank(i % 4).rearrange("p (k n) -> p k n", k=4), ACT.Copy).then_inc(x2t_evac, 1)
            act.wait_ge(s_gd, 1)
            a.activation(gd[:, 1, :], gd[:, 0, :], ACT.Exp).then_inc(s_ge, 1)
            highs(rm, x2nT)

        @block.vector
        def _(dve):
            v = nc.vector
            chain = [0]

            def link(ins):
                chain[0] += 1
                ins.then_inc(s_dchain, 1)
                dve.wait_ge(s_dchain, chain[0])

            dve.wait_ge(s_edges[0], 16)
            link(v.tensor_copy(dpf[:, :], dpi[:, :]))
            dve.wait_ge(s_cst2, 9)
            dve.wait_ge(s_edges[1], 16)
            dve.wait_ge(s_edges[2], 16)
            link(v.tensor_copy(sc[:, :], sci[:, :]))
            link(v.tensor_copy(dc[:, :], dci[:, :]))
            link(v.tensor_reduce(dmin[:, :], dpf[:, :], AX.X, ALU.min))
            link(v.tensor_reduce(dmax[:, :], dpf[:, :], AX.X, ALU.max))
            link(v.tensor_scalar(rel[:, :], bhi[:, :], dmin[:, :], None, ALU.is_ge))
            link(v.scalar_tensor_tensor(out=rel[:, :], in0=blo[:, :], scalar=dmax[:, :], in1=rel[:, :],
                                        op0=ALU.is_le, op1=ALU.mult))
            link(v.tensor_scalar(ext[:, 0:TT], rel[:, :], up[:, :], None, ALU.mult))
            v.tensor_scalar(ext[:, TT:2 * TT], rel[:, :], down[:, :], None, ALU.mult).then_inc(s_ext, 1)
            dve.wait_ge(s_extr, 1)
            link(v.tensor_scalar(rng[:, 0, :], extr[0:1, TT:2 * TT], -1.0, float(PAIRS), ALU.mult, ALU.add))
            link(v.tensor_tensor(rng[:, 1, :], extr[0:1, 0:TT], rng[:, 0, :], ALU.subtract))
            link(v.tensor_scalar(rng[:, 0, :], rng[:, 0, :], float(PAIRS - 1), None, ALU.min))
            link(v.tensor_scalar(rng[:, 1, :], rng[:, 1, :], 1.0, None, ALU.max))
            link(v.memset(rng[:, 3, :], 0.0))
            link(v.tensor_tensor_scan(rng[:, 2, :], rng[:, 1, :], rng[:, 3, :], 0.0, ALU.add, ALU.add))
            link(v.tensor_tensor(rng[:, 3, :], rng[:, 2, :], rng[:, 1, :], ALU.subtract))
            v.tensor_copy(rngi[:, :, :], rng[:, :, :]).then_inc(s_rng, 1)
            dve.wait_ge(s_rng, 1)

            with dve.Fori(0, TT) as b:
                first = dve.value_load(rngi[0:1, 0, ds(b, 1)], min_val=0, max_val=PAIRS - 1)
                count = dve.value_load(rngi[0:1, 1, ds(b, 1)], min_val=1, max_val=PAIRS)
                begin = dve.value_load(rngi[0:1, 3, ds(b, 1)], min_val=0, max_val=PAIRS * TT)
                with dve.Fori(0, count) as i:
                    at = nc.s_assert_within(first + i, 0, PAIRS - 1, skip_runtime_bounds_check_because="first + count is at most PAIRS")
                    side = dve.snap((begin + i) & 1)
                    for p in range(2):
                        col = 2 * at + p
                        dve.wait_ge(oh_free, 2 * (begin + i) + p + 1)
                        v.tensor_scalar(ohd[:, ds(2 * side + p, 1), :].rearrange("p a n -> p (a n)"),
                                        iota[:, ds(b * P, P)], dc[:, ds(col, 1)], None, ALU.is_equal)
                        v.tensor_scalar(ohs[:, ds(2 * side + p, 1), :].rearrange("p a n -> p (a n)"), iota[:, :],
                                        sc[:, ds(col, 1)], None, ALU.is_equal).then_inc(oh_ready, 1)

            dve.wait_ge(s_deg, 1)
            for t in range(TT):
                dve.wait_ge(s_degcol, t)
                v.tensor_tensor_reduce(out=dscr[:, :], in0=PB[:, t * P:(t + 1) * P], in1=ident[:, :], scale=1.0,
                                       scalar=0.0, op0=ALU.mult, op1=ALU.add,
                                       accum_out=deg[:, t:t + 1]).then_inc(s_degcol, 1)
            dve.wait_ge(s_rstd, 1)
            for t in range(TT):
                v.tensor_scalar(xn[:, t, :], xn[:, t, :], negmean[:, t:t + 1], rstd[:, t:t + 1], ALU.add,
                                ALU.mult).then_inc(s_xn, 1)
            dve.wait_ge(s_xn, TT)
            dve.wait_ge(s_dis, 1)
            with dve.Fori(0, KT // 2) as j2:
                for p in range(2):
                    j = 2 * j2
                    dve.wait_ge(ax_evac, j + p + 1)
                    for t in range(TT):
                        ins = v.tensor_scalar(xs[:, p, t, :], xn[:, t, ds((j + p) * P, P)], dis[:, t:t + 1], None, ALU.mult)
                    ins.then_inc(xs_ready, 1)
            dve.wait_ge(s_ad, 1)
            for t in range(TT):
                dve.wait_ge(s_adcol, t)
                v.tensor_tensor_reduce(out=dscr[:, :], in0=PB[:, t * P:(t + 1) * P], in1=ident[:, :], scale=1.0,
                                       scalar=0.0, op0=ALU.mult, op1=ALU.add,
                                       accum_out=adis[:, t:t + 1]).then_inc(s_adcol, 1)

            def rows(r, src, finish):
                def lows(T, p, at):
                    dve.wait_ge(r.high, T + 1)
                    v.tensor_tensor(stl[:, p], src[:, :, at], sth[:, p].bitcast(F32), ALU.subtract).then_inc(r.low, 1)

                lows(0, 0, slice(0, P))
                with dve.Fori(0, r.chunks) as c:
                    with dve.Fori(0, TT // 2 - 1) as g:
                        for p in range(2):
                            T = TT * c + 2 * g + p
                            lows(T + 1, (p + 1) % 2, ds(P * (2 * g + p + 1), P))
                            dve.wait_ge(r.done, T + 1)
                            finish(c, 2 * g + p, p, T, g)
                    for p in range(2):
                        t = TT - 2 + p
                        T = TT * c + t
                        lows(T + 1, (p + 1) % 2, slice((TT - 1) * P, NP) if p == 0 else slice(0, P))
                        dve.wait_ge(r.done, T + 1)
                        finish(c, t, p, T, TT // 2 - 1)

            def finish_graph(c, t, p, T, g):
                dve.wait_ge(g_x[p], 16 * (TT // 2 * c + g + 1))
                dve.wait_ge(g_c, START + T)
                dve.wait_ge(y_ready, START + T)
                v.scalar_tensor_tensor(out=u1[:, :], in0=bgb[:, ds(c * CW, CW)], scalar=adis[:, ds(t, 1)],
                                       in1=bank(6 + p), op0=ALU.mult, op1=ALU.add).then_inc(rg.free, 1)
                dve.wait_ge(rg.free, T + 3)
                v.scalar_tensor_tensor(out=u2[:, :], in0=u1[:, :], scalar=dis[:, ds(t, 1)],
                                       in1=xrow[:, p, :], op0=ALU.mult, op1=ALU.add).then_inc(g_c, 1)
                dve.wait_ge(g_c, START + T + 1)
                dve.wait_ge(g_out[p], START + 16 * (TT // 2 * c + g))
                v.tensor_tensor(yrow[:, p, :], u2[:, :], bob[:, ds(c * CW, CW)], ALU.add).then_inc(y_ready, 1)

            dve.wait_ge(s_bias[3], 16)
            dve.wait_ge(s_bias[4], 16)
            rows(rg, axT, finish_graph)

            for i in range(2 * TT):
                t, k0 = i // 2, 4 * (i % 2)
                dve.wait_ge(xt_high, i + 1)
                if i == 0:
                    graph_over(dve)
                v.tensor_tensor(xl[:, k0:k0 + 4, t * P:(t + 1) * P], bank(i % 4).rearrange("p (k n) -> p k n", k=4),
                                xh[:, k0:k0 + 4, t * P:(t + 1) * P].bitcast(F32), ALU.subtract).then_inc(xt_low, 1)
            dve.wait_ge(a_cst, 4)

            def stack(j, i):
                c0, n = CHUNKS[i % 3]
                dve.wait_ge(qf_ready, 3 + 6 * j + i + 1)
                dve.wait_ge(phi_done, START + 22 * j + (10 if i >= 3 else 0))
                v.tensor_copy(tk[0:64, 0, c0:c0 + n], qf[0:64, 0:n])
                v.tensor_copy(tk[64:128, 1, c0:c0 + n], qf[64:128, 0:n]).then_inc(t_hi, 1)
                dve.wait_ge(t_hi, 6 * j + i + 1)
                v.tensor_tensor(tk[64:128, 0, c0:c0 + n], qf[0:64, 0:n], tk[0:64, 0, c0:c0 + n].bitcast(F32), ALU.subtract)
                v.tensor_tensor(tk[0:64, 1, c0:c0 + n], qf[64:128, 0:n], tk[64:128, 1, c0:c0 + n].bitcast(F32),
                                ALU.subtract).then_inc(t_done, 1)
                dve.wait_ge(s_hi, 6 * j + i + 1)
                v.tensor_tensor(sk[64:128, 0, c0:c0 + n], sqf[0:64, 0:n], sk[0:64, 0, c0:c0 + n].bitcast(F32), ALU.subtract)
                v.tensor_tensor(sk[0:64, 1, c0:c0 + n], sqf[64:128, 0:n], sk[64:128, 1, c0:c0 + n].bitcast(F32),
                                ALU.subtract).then_inc(s_done, 1)

            with dve.Fori(0, KT) as j:
                for i in range(3):
                    stack(j, i)
                dve.wait_ge(kv_done, START + 2 * j)
                for i, (t0, nt) in enumerate(((0, 3), (3, 3), (6, 2), (8, 2))):
                    dve.wait_ge(aux_done, START + 12 * j + i + 1)
                    v.tensor_copy(vt[:, t0:t0 + nt, :, 0:DK],
                                  bank(6 + i % 2, nt * P).rearrange("p (t h d) -> p t h d", t=nt, h=2)).then_inc(aux_evac, 1)
                for h in range(2):
                    for i in range(TT // 2):
                        dve.wait_ge(exp_done, 2 + 22 * j + 5 * h + i + 1)
                        v.tensor_scalar(kphi[:, 2 * i:2 * i + 2, :], kphi[:, 2 * i:2 * i + 2, :], EPS_PHI, None,
                                        ALU.add).then_inc(kph_ready, 1)
                    dve.wait_ge(aux_done, START + 12 * j)
                    dve.wait_ge(kv_done, START + 2 * j + h + 1)
                    v.tensor_copy(kvs[:, h, :, :], bank(5, MH * (DK + 1)).rearrange("p (m d) -> p m d", m=MH)).then_inc(kv_evac, 1)
                for i in range(3, 6):
                    stack(j, i)
                for h in range(2):
                    for i in range(6):
                        c0, n = CHUNKS[i // 2]
                        dve.wait_ge(exp_done, 2 + 22 * j + 10 + 6 * h + i + 1)
                        v.tensor_scalar(qphi[:, i % 2, c0:c0 + n], qphi[:, i % 2, c0:c0 + n], EPS_PHI, None,
                                        ALU.add).then_inc(qph_ready, 1)
                    for i in range(2):
                        f = 4 + 2 * h + i
                        half = bank(6 + f % 2, 5 * (DK + 1)).rearrange("p (t d) -> p t d", t=5)
                        dve.wait_ge(aux_done, START + 12 * j + f + 1)
                        dve.wait_ge(aux_evac, 2 + 12 * j + f)
                        v.reciprocal(rec[:, :], half[:, :, DK:DK + 1].rearrange("p t a -> p (t a)")).then_inc(rec_done, 1)
                        dve.wait_ge(rec_done, 4 * j + 2 * h + i + 1)
                        v.tensor_tensor(att[:, 5 * i:5 * i + 5, DK * h:DK * h + DK], half[:, :, 0:DK],
                                        rec[:, :].rearrange("p (t a) -> p t a", a=1).broadcast_to([P, 5, DK]),
                                        ALU.mult).then_inc(aux_evac, 1)
                for i, (t0, nt) in enumerate(((0, 3), (3, 3), (6, 2), (8, 2))):
                    dve.wait_ge(aux_done, START + 12 * j + 8 + i + 1)
                    v.tensor_copy(attnT[:, ds(j, 1), t0 * P:(t0 + nt) * P].rearrange("p a n -> p (a n)"),
                                  bank(6 + i % 2, nt * P)).then_inc(aux_evac, 1)

            def finish_residual(c, t, p, T, g):
                dve.wait_ge(o_y[p], 16 * (TT // 2 * c + g + 1))
                v.tensor_tensor(x2[:, ds(t, 1), ds(c * CW, CW)].rearrange("p a n -> p (a n)"), bank(6 + p),
                                yrow[:, p, :], ALU.add).then_inc(ro.free, 1)

            attention_over(dve)
            rows(ro, attnT, finish_residual)

            dve.wait_ge(ro.free, NC * TT + 2)
            for t in range(TT):
                dve.wait_ge(s_mean, t)
                for c in range(NC):
                    ins = v.bn_stats(stats[:, c, :], x2[:, t, c * CW:(c + 1) * CW])
                    link(ins)
                v.bn_aggr(aggr[:, t, :], stats[:, :, :]).then_inc(s_mean, 1)
            dve.wait_ge(s_rstd2, 2)
            for t in range(TT):
                if t >= 2:
                    dve.wait_ge(x2t_done, 2 * (t - 1))
                v.tensor_scalar(xhat[:, t % 2, :], x2[:, t, :], aggr[:, t, 0:1], rstd[:, t:t + 1], ALU.subtract,
                                ALU.mult).then_inc(s_xhat, 1)

            dve.wait_ge(s_bias[6], 16)
            for i, (c0, n) in enumerate(CHUNKS):
                dve.wait_ge(lg_done, i + 1)
                v.tensor_scalar(lgT[:, c0:c0 + n], bank(3 + i, n)[0:E, :], gb[:, :], None, ALU.add).then_inc(lg_evac, 1)
            dve.wait_ge(lgt_done, 1)
            link(v.tensor_copy(lg[:, :, :], bank(0, TT * E).rearrange("p (t e) -> p t e", t=TT)))
            for t in range(TT):
                link(v.max(mx[:, t, :], lg[:, t, :]))
                link(v.max_index(ix[:, t, :], mx[:, t, :], lg[:, t, :]))
            link(v.tensor_copy(ixf[:, :, :], ix[:, :, :]))
            v.tensor_tensor(gd[:, 0, :], mx[:, :, 1:2].rearrange("p t a -> p (t a)"),
                            mx[:, :, 0:1].rearrange("p t a -> p (t a)"), ALU.subtract).then_inc(s_gd, 1)
            dve.wait_ge(s_ge, 1)
            link(v.tensor_scalar(gd[:, 3, :], gd[:, 1, :], 1.0, None, ALU.add))
            link(v.reciprocal(gd[:, 2, :], gd[:, 3, :]))
            link(v.tensor_tensor(gd[:, 3, :], gd[:, 1, :], gd[:, 2, :], ALU.mult))
            dve.wait_ge(s_gate, 1)
            for t in range(TT):
                link(v.tensor_scalar(gate[:, t, :], iota8[:, :], ixf[:, t, 0:1], gd[:, 2, t:t + 1], ALU.is_equal, ALU.mult))
                link(v.tensor_scalar(gate2[:, t, :], iota8[:, :], ixf[:, t, 1:2], gd[:, 3, t:t + 1], ALU.is_equal, ALU.mult))
            v.tensor_tensor(gate[:, :, :], gate[:, :, :], gate2[:, :, :], ALU.add).then_inc(s_gate, 1)
            for i in range(TT):
                dve.wait_ge(gt_done, i + 1)
                v.tensor_copy(gateT[:, i * P:(i + 1) * P], bank(i % 2, P)[0:E, :]).then_inc(gt_evac, 1)
            for i in range(TT * NC):
                dve.wait_ge(eb_done, i + 1)
                t, c = i // NC, i % NC
                v.tensor_tensor(x2[:, t, c * CW:(c + 1) * CW], x2[:, t, c * CW:(c + 1) * CW], bank(2 + i % 2),
                                ALU.add).then_inc(eb_evac, 1)
            dve.wait_ge(eb_evac, TT * NC)

            def finish_expert(c, t, p, T, g):
                acc = x2[:, ds(t, 1), ds((c & 1) * CW, CW)].rearrange("p a n -> p (a n)")
                e = nc.s_assert_within(c >> 1, 0, E - 1, skip_runtime_bounds_check_because="c is under 2 E")
                v.scalar_tensor_tensor(out=acc, in0=bank(6 + p), scalar=gate[:, ds(t, 1), ds(e, 1)].rearrange("p a n -> p (a n)"),
                                       in1=acc, op0=ALU.mult, op1=ALU.add).then_inc(rm.free, 1)

            rows(rm, x2nT, finish_expert)

        @block.tensor
        def _(pe):
            mm = nc.tensor.matmul
            pe.wait_ge(s_rng, 1)
            pe.wait_ge(s_cst2, 9)
            with pe.Fori(0, TT // 2) as b2:
                for s in range(2):
                    b = 2 * b2 + s
                    first = pe.value_load(rngi[0:1, 0, ds(b, 1)], min_val=0, max_val=PAIRS - 1)
                    count = pe.value_load(rngi[0:1, 1, ds(b, 1)], min_val=1, max_val=PAIRS)
                    begin = pe.value_load(rngi[0:1, 3, ds(b, 1)], min_val=0, max_val=PAIRS * TT)
                    pe.wait_ge(at_evac, b + 1)
                    for c0, n in CHUNKS:
                        mm(PB[:, 1536 * s + c0:1536 * s + c0 + n], diag[:, NP - P:NP],
                           diag[:, ds(NP - P - P * b + c0, n)], start=True, stop=False, skip_group_check=True)
                    with pe.Fori(0, count) as i:
                        side = pe.snap((begin + i) & 1)
                        for p in range(2):
                            pe.wait_ge(oh_ready, 2 * (begin + i) + p + 1)
                            for c0, n in CHUNKS:
                                ins = mm(PB[:, 1536 * s + c0:1536 * s + c0 + n],
                                         ohd[:, ds(2 * side + p, 1), :].rearrange("p a n -> p (a n)"),
                                         ohs[:, ds(2 * side + p, 1), c0:c0 + n].rearrange("p a n -> p (a n)"),
                                         start=False, stop=False, skip_group_check=True)
                            ins.then_inc(oh_free, 1)
                    for c0, n in CHUNKS:
                        ins = mm(PB[:, 1536 * s + c0:1536 * s + c0 + 2], diag[:, NP - P:NP], diag[:, 0:2],
                                 start=False, stop=True, skip_group_check=True)
                    ins.then_inc(at_done, 1)

            pe.wait_ge(s_pchain, TT + 1)
            pe.wait_ge(at_evac, TT + 2)
            for c0, n in CHUNKS:
                ins = mm(PB[:, c0:c0 + n], ones[:, :], degacc[:, c0:c0 + n], start=True, stop=True)
            ins.then_inc(s_deg, 1)
            with pe.Fori(0, KT // 2) as j2:
                for s in range(2):
                    j = 2 * j2
                    pe.wait_ge(xs_ready, j + s + 1)
                    pe.wait_ge(ax_evac, j + s + 1)
                    for c0, n in CHUNKS:
                        for t in range(TT):
                            ins = mm(PB[:, 1536 * s + c0:1536 * s + c0 + n], xs[:, s, t, :], AT[:, t, c0:c0 + n],
                                     start=(t == 0), stop=(t == TT - 1))
                    ins.then_inc(ax_done, 1)
            pe.wait_ge(s_pchain, 3 * TT + 2)
            pe.wait_ge(ax_evac, KT + 2)
            for c0, n in CHUNKS:
                ins = mm(PB[:, c0:c0 + n], ones[:, :], degacc[:, c0:c0 + n], start=True, stop=True)
            ins.then_inc(s_ad, 1)

            def rows(r):
                with pe.Fori(0, r.chunks) as c:
                    pe.wait_ge(r.wready, KT * (c + 1))
                    apart(pe)
                    cp = c & 1
                    with pe.Fori(0, TT // 2) as g:
                        for p in range(2):
                            T = TT * c + 2 * g + p
                            pe.wait_ge(r.low, T + 1)
                            pe.wait_ge(r.free, T + 1)
                            for k in range(KT):
                                high = wh[:, ds(cp, 1), k, :].rearrange("p a n -> p (a n)")
                                lowr = wl[:, ds(cp, 1), k, :].rearrange("p a n -> p (a n)")
                                mm(bank(6 + p), sth[:, p, k, :], high, start=(k == 0), stop=False)
                                mm(bank(6 + p), sth[:, p, k, :], lowr, start=False, stop=False)
                                ins = mm(bank(6 + p), stl[:, p, k, :], high, start=False, stop=(k == KT - 1))
                            ins.then_inc(r.done, 1)

            rows(rg)

            for i in range(2 * TT):
                t = i // 2
                if i >= 4:
                    pe.wait_ge(xt_low, i - 3)
                for q in range(4):
                    k = 4 * (i % 2) + q
                    ins = nc.tensor.transpose(bank(i % 4)[:, q * P:(q + 1) * P], xn[:, t, k * P:(k + 1) * P], ident[:, :])
                ins.then_inc(xt_done, 1)
            pe.wait_ge(xt_low, 2 * TT)
            pe.wait_ge(a_cst, 4)

            def project(j, wi):
                pe.wait_ge(a_w, START + 3 * j + wi + 1)
                for i, (c0, n) in enumerate(CHUNKS):
                    if wi == 0:
                        pe.wait_ge(qf_ready, 6 * j + i + 1)
                    elif wi == 1:
                        pe.wait_ge(qf_ready, 3 + 6 * j + i + 1)
                    else:
                        pe.wait_ge(vt_ready, 3 * j + i + 1)
                    for k in range(KT):
                        mm(bank(i, n), hw[:, wi, 0, k, :], xh[:, k, c0:c0 + n], start=(k == 0), stop=False)
                        mm(bank(i, n), hw[:, wi, 0, k, :], xl[:, k, c0:c0 + n], start=False, stop=False)
                        ins = mm(bank(i, n), hw[:, wi, 1, k, :], xh[:, k, c0:c0 + n], start=False, stop=(k == KT - 1))
                    ins.then_inc(proj_done, 1)

            with pe.Fori(0, KT) as j:
                project(j, 0)
                project(j, 1)
                for i, (t0, nt) in enumerate(((0, 3), (3, 3), (6, 2), (8, 2))):
                    pe.wait_ge(aux_evac, 12 * j + i + 1)
                    pe.wait_ge(vt_ready, 3 * j + (1, 2, 2, 3)[i])
                    for q in range(nt):
                        ins = nc.tensor.transpose(bank(6 + i % 2)[:, q * P:(q + 1) * P],
                                                  vT[:, (t0 + q) * P:(t0 + q + 1) * P], ident[:, :])
                    ins.then_inc(aux_done, 1)

                def key_features(h, i):
                    f = 5 * h + i
                    pe.wait_ge(exp_done, 22 * j + f + 1)
                    for q in range(2):
                        at = slice((2 * i + q) * P, (2 * i + q + 1) * P)
                        o = bank(3 + f % 2)[:, q * M:(q + 1) * M]
                        mm(o, tk[:, h, at], orfh[:, :], start=True, stop=False)
                        mm(o, tk[:, h, at], orfl[:, :], start=False, stop=False)
                        ins = mm(o, sk[:, h, at], negr[:, :], start=False, stop=True)
                    ins.then_inc(phi_done, 1)

                def key_values(h):
                    pe.wait_ge(kv_evac, START + 2 * j + h)
                    pe.wait_ge(kph_ready, 10 * j + 5 * h + 5)
                    pe.wait_ge(aux_evac, 2 + 12 * j + 4)
                    for m in range(MH):
                        for t in range(TT):
                            n = LAST if t == TT - 1 else P
                            ins = mm(bank(5)[:, m * (DK + 1):(m + 1) * (DK + 1)], kphi[0:n, t, m * P:(m + 1) * P],
                                     vt[0:n, t, h, :], start=(t == 0), stop=(t == TT - 1))
                    ins.then_inc(kv_done, 1)

                def query_features(h, i):
                    f = 10 + 6 * h + i
                    m = slice(i % 2 * P, i % 2 * P + P)
                    c0, n = CHUNKS[i // 2]
                    pe.wait_ge(exp_done, 22 * j + f + 1)
                    mm(bank(3 + f % 2, n), orfh[:, m], tk[:, h, c0:c0 + n], start=True, stop=False)
                    mm(bank(3 + f % 2, n), orfl[:, m], tk[:, h, c0:c0 + n], start=False, stop=False)
                    mm(bank(3 + f % 2, n), negr[:, m], sk[:, h, c0:c0 + n], start=False, stop=True).then_inc(phi_done, 1)

                def outputs(h, i):
                    f = 4 + 2 * h + i
                    pe.wait_ge(aux_evac, 12 * j + f + 1)
                    pe.wait_ge(qph_ready, 12 * j + 6 * h + (4 if i == 0 else 6))
                    for q in range(5):
                        t = 5 * i + q
                        for m in range(MH):
                            ins = mm(bank(6 + f % 2)[:, q * (DK + 1):(q + 1) * (DK + 1)],
                                     qphi[:, m, t * P:(t + 1) * P], kvs[:, h, m, :], start=(m == 0), stop=(m == MH - 1))
                    ins.then_inc(aux_done, 1)

                pe.wait_ge(t_done, START + 6 * j + 3)
                pe.wait_ge(s_done, START + 6 * j + 3)
                for i in range(TT // 2):
                    key_features(0, i)
                key_features(1, 0)
                key_values(0)
                for i in range(1, TT // 2):
                    key_features(1, i)
                project(j, 2)
                key_values(1)
                pe.wait_ge(t_done, START + 6 * j + 6)
                pe.wait_ge(s_done, START + 6 * j + 6)
                for i in range(6):
                    query_features(0, i)
                query_features(1, 0)
                pe.wait_ge(kv_evac, START + 2 * j + 1)
                outputs(0, 0)
                query_features(1, 1)
                outputs(0, 1)
                for i in range(2, 6):
                    query_features(1, i)
                pe.wait_ge(kv_evac, START + 2 * j + 2)
                outputs(1, 0)
                outputs(1, 1)
                for i, (t0, nt) in enumerate(((0, 3), (3, 3), (6, 2), (8, 2))):
                    pe.wait_ge(aux_evac, 12 * j + 8 + i + 1)
                    for q in range(nt):
                        ins = nc.tensor.transpose(bank(6 + i % 2)[:, q * P:(q + 1) * P], att[:, t0 + q, :], ident[:, :])
                    ins.then_inc(aux_done, 1)

            rows(ro)

            for i in range(2 * TT):
                t = i // 2
                pe.wait_ge(s_xhat, t + 1)
                if i >= 4:
                    pe.wait_ge(x2t_evac, i - 3)
                for q in range(4):
                    k = 4 * (i % 2) + q
                    ins = nc.tensor.transpose(bank(i % 4)[:, q * P:(q + 1) * P], xhat[:, t % 2, k * P:(k + 1) * P], ident[:, :])
                ins.then_inc(x2t_done, 1)
            pe.wait_ge(x2t_evac, 2 * TT)
            pe.wait_ge(s_bias[5], 16)
            for i, (c0, n) in enumerate(CHUNKS):
                for k in range(KT):
                    ins = mm(bank(3 + i, n)[0:E, :], gw[:, k, :], x2nT[:, k, c0:c0 + n], start=(k == 0), stop=(k == KT - 1))
                ins.then_inc(lg_done, 1)
            pe.wait_ge(lg_evac, len(CHUNKS))
            for t in range(TT):
                ins = nc.tensor.transpose(bank(0)[:, t * E:(t + 1) * E], lgT[:, t * P:(t + 1) * P], ident[0:E, 0:E])
            ins.then_inc(lgt_done, 1)
            pe.wait_ge(s_gate, 2)
            for t in range(TT):
                if t >= 2:
                    pe.wait_ge(gt_evac, t - 1)
                nc.tensor.transpose(bank(t % 2, P)[0:E, :], gate[:, t, :], ident[:, :]).then_inc(gt_done, 1)
            pe.wait_ge(gt_evac, TT)
            pe.wait_ge(s_bias[7], 16)
            for i in range(TT * NC):
                t, c = i // NC, i % NC
                if i >= 2:
                    pe.wait_ge(eb_evac, i - 1)
                mm(bank(2 + i % 2), gateT[:, t * P:(t + 1) * P], eb[:, c * CW:(c + 1) * CW], start=True,
                   stop=True).then_inc(eb_done, 1)
            rows(rm)



_INS = ["x", "dst_pairs", "src_cols", "dst_cols", "wg", "bg", "wq", "bq", "wk", "bk", "wv", "bv", "wo", "bo", "orf",
        "gate_w", "gate_b", "expert_w", "expert_b"]


def kernel(**inputs):
    import numpy as np
    import concourse.bacc as bacc
    from concourse.bass_utils import run_bass_kernel_spmd

    a = {k: np.asarray(v) for k, v in inputs.items()}

    def chunks(w):
        return w.reshape(KT, P, NC, CW).transpose(2, 0, 1, 3)

    def heads(w):
        return w.T.reshape(KT, P, KT, P).transpose(2, 1, 0, 3)

    def column(b):
        return b.reshape(KT, P).T

    slots = 2 * PAIRS * P
    src = np.pad(a["src"], (0, slots - EDGES), constant_values=-1)
    dst = np.pad(a["dst"], (0, slots - EDGES), mode="edge")
    orfT = a["L0_mix_orf"].T
    arrays = {
        "x": np.pad(a["x"], ((0, NP - N), (0, 0))),
        "dst_pairs": dst.reshape(PAIRS, PAIR),
        "src_cols": src.reshape(2 * PAIRS, P).T,
        "dst_cols": dst.reshape(2 * PAIRS, P).T,
        "wg": chunks(a["L0_gnn_W"].T),
        "bg": a["L0_gnn_b"].reshape(1, D),
        "wq": heads(a["L0_mix_Wq"]), "bq": column(a["L0_mix_bq"]),
        "wk": heads(a["L0_mix_Wk"]), "bk": column(a["L0_mix_bk"]),
        "wv": heads(a["L0_mix_Wv"]), "bv": column(a["L0_mix_bv"]),
        "wo": chunks(a["L0_mix_Wo"].T),
        "bo": a["L0_mix_bo"].reshape(1, D),
        "orf": np.concatenate([orfT, orfT], axis=0),
        "gate_w": a["L0_ffn_gate_w"].T.reshape(KT, P, E).transpose(1, 0, 2),
        "gate_b": a["L0_ffn_gate_b"].reshape(E, 1),
        "expert_w": a["L0_ffn_expert_w"].reshape(E, KT, P, NC, CW).transpose(0, 3, 1, 2, 4).reshape(E * NC, KT, P, CW),
        "expert_b": a["L0_ffn_expert_b"],
    }
    nc = bacc.Bacc("TRN2", target_bir_lowering=False, num_devices=1)
    given, args = {}, []
    for name in _INS:
        given[name] = np.ascontiguousarray(arrays[name])
        args.append(nc.dram_tensor(name, given[name].shape, mybir.dt.from_np(given[name].dtype), kind="ExternalInput").ap())
    out = nc.dram_tensor("out", (N, D), F32, kind="ExternalOutput").ap()
    gps_layer(nc, *args, out)
    r = run_bass_kernel_spmd(nc, [given], core_ids=[0])
    return r.results[0]["out"]
```

```python
from contextlib import ExitStack

import concourse.bass as bass
from concourse import mybir

P = 128
N, D = 1250, 1024
TT = -(-N // P)
NP = TT * P
LAST = N - (TT - 1) * P
KT = D // P
CW = 512
NC = D // CW
H, DK, M = 16, 64, 256
MH = M // P
E = 8
EDGES = 20000
PAIR = 2 * P
PAIRS = -(-EDGES // PAIR) + 1
MAXT = (2 * N + 2 * (P - 1)) // P + 1 + 2 * (E - 2) + 1
CHUNKS = ((0, 512), (512, 512), (1024, NP - 1024))
EPS_LN = 1e-5
EPS_PHI = 1e-6
START = 1
PHI_SCALE = float(DK) ** -0.25
SQ_SCALE = (1.0 / (2.0 * DK ** 0.5) / PHI_SCALE) ** 0.5

ALU = mybir.AluOpType
ACT = mybir.ActivationFunctionType
AX = mybir.AxisListType
F32 = mybir.dt.float32
F32R = mybir.dt.float32r
BF16 = mybir.dt.bfloat16
F16 = mybir.dt.float16
I32 = mybir.dt.int32
U32 = mybir.dt.uint32
ds = bass.ds
RMAX = bass.bass_isa.ReduceOp.max


def gps_layer(nc, x, dst_pairs, src_cols, dst_cols, wg, bg, wq, bq, wk, bk, wv, bv, wo, bo, orf,
              gate_w, gate_b, expert_w, expert_b, out):
    x2n_half = [nc.dram_tensor(f"x2n_half{c}", [NP, CW], F32, kind="Internal").ap() for c in range(NC)]
    slot_y = nc.dram_tensor("slot_y", [MAXT * P, D], F32, kind="Internal").ap()
    y1 = nc.dram_tensor("y1_scratch", [NC, TT, P, CW], F32, kind="Internal").ap()
    ctx = ExitStack()
    with ctx:
        def sem(name):
            return ctx.enter_context(nc.semaphore(name))

        def keep(name, shape, dt, where=ctx):
            return where.enter_context(nc.sbuf_tensor(name, shape, dt))

        ident = keep("ident", [P, P], F32)
        ones = keep("ones", [P, P], F32)
        dis = keep("dis", [P, TT], F32)
        adis = keep("adis", [P, TT], F32)
        sums = keep("sums", [P, TT], F32)
        negmean = keep("negmean", [P, TT], F32)
        ssq = keep("ssq", [P, TT], F32)
        varx = keep("varx", [P, TT], F32)
        rstd = keep("rstd", [P, TT], F32)
        mhalf = keep("mhalf", [P, TT], F32)
        deg = keep("deg", [P, TT], F32)
        biasT = keep("biasT", [P, 3, KT], F32)
        PB = ctx.enter_context(nc.psum_tensor("PB", [P, 8 * 512], F32))

        s0 = ExitStack()
        xn = keep("xn", [P, TT, D], F32, s0)
        s0.close()
        s0 = ExitStack()
        attnT = keep("attnT", [P, KT, NP], F32, s0)
        s0.close()
        s0 = ExitStack()
        xg = keep("xg", [P, NC, CW], F32, s0)
        s1 = ExitStack()
        mwh1 = keep("mwh1", [P, KT, D], F32R, s1)
        s1.close()
        s1 = ExitStack()
        xhat = keep("xhat", [P, 2, D], F32, s1)
        x2T = keep("x2T", [P, 2, KT, P], F32, s1)
        gw = keep("gw", [P, KT, E], F32, s1)
        gb = keep("gb", [P, E], F32, s1)
        hotr = keep("hotr", [P, 2 * TT, P], F32, s1)
        hota = keep("hota", [P, 2 * TT, MAXT], F32, s1)
        hott = keep("hott", [P, 2 * TT, MAXT], F32, s1)
        s1.close()
        s0.close()
        slot0 = keep("slot0", [P, D * TT], F32)

        pa = ExitStack()
        xh = keep("xh", [P, KT, NP], F32R, pa)
        xl = keep("xl", [P, KT, NP], F32R, pa)
        hw = keep("hw", [P, 3, 2, KT, P], F32R, pa)
        hraw = keep("hraw", [P, KT, P], F32, pa)
        tk = keep("tk", [P, 2, NP], F32R, pa)
        sk = keep("sk", [P, 2, NP], F32R, pa)
        qphi = keep("qphi", [P, MH, NP], F32, pa)
        vT = qphi[:, 0, :]
        kphi = keep("kphi", [P, TT, M], F32, pa)
        att = kphi[:, :, 0:P]
        vt = keep("vt", [P, TT, 2, DK + 1], F32, pa)
        qf = keep("qf", [P, CW], F32, pa)
        sqf = keep("sqf", [P, CW], F32, pa)
        kvs = keep("kvs", [P, 2, MH, DK + 1], F32, pa)
        rec = keep("rec", [P, TT // 2], F32, pa)
        orfh = keep("orfh", [P, M], F32R, pa)
        orfl = keep("orfl", [P, M], F32R, pa)
        negr = keep("negr", [P, M], F32R, pa)
        pa.close()

        s1 = ExitStack()
        axT = keep("axT", [P, KT, NP], F32, s1)
        s1.close()
        x2 = keep("x2", [P, TT, D], F32)

        pg = ExitStack()
        AT = keep("AT", [P, TT, NP], F32, pg)
        xs = keep("xs", [P, 2, TT, P], F32, pg)
        iota = keep("iota", [P, NP], F16, pg)
        diag = keep("diag", [P, 2 * NP - P], BF16, pg)
        ohs = keep("ohs", [P, 4, NP], BF16, pg)
        ohd = keep("ohd", [P, 4, P], BF16, pg)
        degacc = keep("degacc", [P, NP], F32, pg)
        sci = keep("sci", [P, 2 * PAIRS], I32, pg)
        dci = keep("dci", [P, 2 * PAIRS], I32, pg)
        sc = keep("sc", [P, 2 * PAIRS], F32, pg)
        dc = keep("dc", [P, 2 * PAIRS], F32, pg)
        dpi = keep("dpi", [PAIRS, PAIR], I32, pg)
        dpf = keep("dpf", [PAIRS, PAIR], F32, pg)
        dmin = keep("dmin", [PAIRS, 1], F32, pg)
        dmax = keep("dmax", [PAIRS, 1], F32, pg)
        blo = keep("blo", [PAIRS, TT], F32, pg)
        bhi = keep("bhi", [PAIRS, TT], F32, pg)
        up = keep("up", [PAIRS, 1], F32, pg)
        down = keep("down", [PAIRS, 1], F32, pg)
        rel = keep("rel", [PAIRS, TT], F32, pg)
        ext = keep("ext", [PAIRS, 2 * TT], F32, pg)
        extr = keep("extr", [PAIRS, 2 * TT], F32, pg)
        rng = keep("rng", [1, 4, TT], F32, pg)
        rngi = keep("rngi", [1, 4, TT], I32, pg)
        junk = keep("junk", [P, D], F32, pg)
        dscr = keep("dscr", [P, P], F32, pg)
        scaled = keep("scaled", [P, NP], F32, pg)
        pg.close()

        pr = ExitStack()
        wh = keep("wh", [P, 2, KT, CW], F32R, pr)
        wl = keep("wl", [P, 2, KT, CW], F32R, pr)
        raw = keep("raw", [P, 4, CW], F32, pr)
        sth = keep("sth", [P, 2, KT, P], F32R, pr)
        stl = keep("stl", [P, 2, KT, P], F32R, pr)
        yrow = keep("yrow", [P, 2, CW], F32, pr)
        xrow = keep("xrow", [P, 2, CW], F32, pr)
        bgb = keep("bgb", [P, D], F32, pr)
        bob = keep("bob", [P, D], F32, pr)
        u1 = keep("u1", [P, CW], F32, pr)
        u2 = keep("u2", [P, CW], F32, pr)
        pr.close()

        pc = ExitStack()
        gathered = keep("gathered", [P, 2 * KT, D], F32, pc)
        pc.close()
        mwh0 = keep("mwh0", [P, KT, D], F32R)
        pw = ExitStack()
        mraw = [keep(f"mraw{i}", [P, KT, D], F32, pw) for i in range(2)]
        pw.close()
        mwl0 = keep("mwl0", [P, KT, D], F32R)
        mwl1 = keep("mwl1", [P, KT, D], F32R)
        mwh, mwl = (mwh0, mwh1), (mwl0, mwl1)
        mth = keep("mth", [P, KT, P], F32R)
        mtl = keep("mtl", [P, KT, P], F32R)
        ybuf = keep("ybuf", [P, NC, CW], F32)
        ebb = keep("ebb", [P, D], F32)
        stats = keep("stats", [P, TT, NC, 6], F32)
        aggr = keep("aggr", [P, TT, 2], F32)
        lg = keep("lg", [P, TT, E], F32)
        mx = keep("mx", [P, TT, 8], F32)
        ix = keep("ix", [P, TT, 8], U32)
        ixf = keep("ixf", [P, TT, 8], F32)
        gd = keep("gd", [P, 4, TT], F32)
        ab = keep("ab", [P, 2, TT], F32)
        sel = keep("sel", [P, 2, TT], F32)
        gab = keep("gab", [P, 3, 2, TT], F32)
        iota8 = keep("iota8", [P, TT, E], F32)
        oneh = keep("oneh", [P, 2, TT, E], F32)
        both = keep("both", [P, TT, E], F32)
        upper = keep("upper", [P, P], F32)
        thr = keep("thr", [P, E, TT], F32)
        over = keep("over", [P, E, TT], F32)
        cnt = keep("cnt", [P, 4, E], F32)
        tot = keep("tot", [P, TT, E], F32)
        carry = keep("carry", [P, TT, E], F32)
        cnti = keep("cnti", [1, 4, E], I32)
        posf = keep("posf", [P, 2, TT], F32)
        pos = keep("pos", [P, 2, TT], I32)
        token = keep("token", [P, TT], F32)
        posa = keep("posa", [P, 2 * TT], F32)
        posr = keep("posr", [P, 2 * TT], F32)
        nums = keep("nums", [P, P], F32)
        starts = keep("starts", [P, MAXT], F32)
        slots = keep("slots", [P, MAXT], I32)
        here = keep("here", [P, NC], I32)

        def bank(b, n=CW):
            return PB[:, 512 * b:512 * b + n]

        s_edges = [sem(f"s_edges{i}") for i in range(3)]
        s_x = [sem(f"s_x{t}") for t in range(TT)]
        s_bias = [sem(f"s_bias{i}") for i in range(10)]
        s_const = sem("s_const")
        s_apart = {e.engine: sem(f"s_apart{n}") for n, e in enumerate((nc.scalar, nc.gpsimd, nc.tensor))}
        s_cst2 = sem("s_cst2")
        s_dchain = sem("s_dchain")
        s_ext = sem("s_ext")
        s_extr = sem("s_extr")
        s_rng = sem("s_rng")
        oh_ready = sem("oh_ready")
        oh_free = sem("oh_free")
        at_done = sem("at_done")
        at_evac = sem("at_evac")
        ln_a = sem("ln_a")
        s_degacc = sem("s_degacc")
        s_deg = sem("s_deg")
        s_degcol = sem("s_degcol")
        s_dis = sem("s_dis")
        s_rstd = sem("s_rstd")
        s_pchain = sem("s_pchain")
        s_xn = sem("s_xn")
        xs_ready = sem("xs_ready")
        ax_done = sem("ax_done")
        ax_evac = sem("ax_evac")
        s_ad = sem("s_ad")
        s_adcol = sem("s_adcol")

        class Rows:
            def __init__(self, name, chunks):
                self.chunks = chunks
                self.raw = [sem(f"{name}_raw{i}") for i in range(4)]
                self.whigh = sem(f"{name}_whigh")
                self.wready = sem(f"{name}_wready")
                self.high = sem(f"{name}_high")
                self.low = sem(f"{name}_low")
                self.done = sem(f"{name}_done")
                self.free = sem(f"{name}_free")

        rg, ro = Rows("rg", NC), Rows("ro", NC)
        g_x = [sem(f"g_x{i}") for i in range(2)]
        g_c = sem("g_c")
        g_out = [sem(f"g_out{i}") for i in range(2)]
        o_y = [sem(f"o_y{i}") for i in range(2)]
        xt_done = sem("xt_done")
        xt_high = sem("xt_high")
        xt_low = sem("xt_low")
        a_raw = sem("a_raw")
        a_high = sem("a_high")
        a_w = sem("a_w")
        a_orf = sem("a_orf")
        a_cst = sem("a_cst")
        proj_done = sem("proj_done")
        qf_ready = sem("qf_ready")
        sq_ready = sem("sq_ready")
        vt_ready = sem("vt_ready")
        t_hi = sem("t_hi")
        t_done = sem("t_done")
        s_hi = sem("s_hi")
        s_done = sem("s_done")
        phi_done = sem("phi_done")
        exp_done = sem("exp_done")
        kph_ready = sem("kph_ready")
        qph_ready = sem("qph_ready")
        kv_done = sem("kv_done")
        kv_evac = sem("kv_evac")
        aux_done = sem("aux_done")
        aux_evac = sem("aux_evac")
        rec_done = sem("rec_done")
        y_ready = sem("y_ready")
        s_stats = sem("s_stats")
        s_mean = sem("s_mean")
        s_rstd2 = sem("s_rstd2")
        s_xhat = sem("s_xhat")
        x2t_done = sem("x2t_done")
        x2t_evac = sem("x2t_evac")
        x2n_stored = [sem(f"x2n_stored{i}") for i in range(2)]
        lg_done = sem("lg_done")
        s_gd = sem("s_gd")
        s_ge = sem("s_ge")
        s_route_const = sem("s_route_const")
        s_both = sem("s_both")
        ranks_done = sem("ranks_done")
        s_cnti = sem("s_cnti")
        s_pos = sem("s_pos")
        slot_hot = sem("slot_hot")
        slots_filled = sem("slots_filled")
        slots_done = sem("slots_done")
        slots_ready = sem("slots_ready")
        here_ready = sem("here_ready")
        xg_ready = [sem(f"xg_ready{i}") for i in range(NC)]
        mt_trans = sem("mt_trans")
        mt_high = sem("mt_high")
        mt_low = sem("mt_low")
        mw_raw = [sem(f"mw_raw{k}") for k in range(KT)]
        mw_high = sem("mw_high")
        mw_ready = sem("mw_ready")
        eb_ready = sem("eb_ready")
        prod_done = sem("prod_done")
        y_copied = [sem(f"y_copied{c}") for c in range(NC)]
        y_stored = [sem(f"y_stored{c}") for c in range(NC)]
        z_stored = [sem(f"z_stored{c}") for c in range(NC)]
        a_gathered = sem("a_gathered")
        b_gathered = [sem(f"b_gathered{i}") for i in range(TT // 2)]
        comb_a = sem("comb_a")
        comb_b = sem("comb_b")
        s_out = sem("s_out")

        block = ctx.enter_context(nc.Block())

        def apart(eng):
            eng.sem_inc(s_apart[eng.engine], 1)

        def tiles(eng, e):
            more = eng.value_load(cnti[0:1, 0, ds(e, 1)], min_val=1, max_val=TT - 1)
            begin = eng.value_load(cnti[0:1, 3, ds(e, 1)], min_val=0, max_val=MAXT - 1)
            return more, begin

        def tile_of(T):
            return nc.s_assert_within(T, 0, MAXT - 1, skip_runtime_bounds_check_because="MAXT bounds the tiles")

        def pairs(eng, pair):
            with eng.Fori(0, KT - 1) as j:
                pair(nc.s_assert_within(j, 0, KT - 2, skip_runtime_bounds_check_because="the loop's bound"), False)
            pair(KT - 1, True)

        def experts(eng, expert):
            with eng.Fori(0, E // 2 - 1) as e2:
                for par in range(2):
                    expert(nc.s_assert_within(2 * e2 + par, 0, E - 3, skip_runtime_bounds_check_because="a pair below the last"), par, False)
            for par in range(2):
                expert(E - 2 + par, par, par == 1)

        def graph_over(eng):
            eng.wait_ge(y_ready, START + NC * TT)
            eng.wait_ge(rg.high, NC * TT + 2)
            eng.wait_ge(rg.low, NC * TT + 1)
            for i in range(2):
                eng.wait_ge(g_out[i], START + 16 * NC * TT // 2)

        def attention_over(eng):
            eng.wait_ge(aux_evac, 12 * KT + 2)

        @block.sync
        def _(sp):
            sp.dma_start(dpi[:, :], dst_pairs).then_inc(s_edges[0], 16)
            sp.dma_start(sci[:, :], src_cols).then_inc(s_edges[1], 16)
            sp.dma_start(dci[:, :], dst_cols).then_inc(s_edges[2], 16)
            for t in range(TT):
                sp.dma_start(xn[:, t, :], x[t * P:(t + 1) * P, :]).then_inc(s_x[t], 16)
            for r0 in range(0, MAXT * P, NP):
                n = min(NP, MAXT * P - r0)
                sp.dma_start(slot_y[r0:r0 + n, :], x[0:n, :]).then_inc(slots_filled, 16)
            for i, b in enumerate((bk, bv, bq)):
                sp.dma_start(biasT[:, i, :], b).then_inc(s_bias[i], 16)

            def load_weights(r, w):
                for i in range(4):
                    sp.dma_start(raw[:, i, :], w[i // KT, i % KT]).then_inc(r.raw[i], 16)
                with sp.Fori(1, r.chunks * KT // 4) as g:
                    for i in range(4):
                        sp.wait_ge(r.wready, 4 * g - 3 + i)
                        s = 4 * g + i
                        sp.dma_start(raw[:, i, :], w.rearrange("c k p n -> (c k) p n")[ds(s, 1)].rearrange("a p n -> (a p) n")).then_inc(r.raw[i], 16)

            sp.wait_ge(ax_done, KT)
            sp.wait_ge(ax_evac, KT + 2)
            sp.wait_ge(s_adcol, TT)
            sp.dma_start(bgb[:, :], bg.broadcast_to([P, D])).then_inc(s_bias[3], 16)
            sp.dma_start(bob[:, :], bo.broadcast_to([P, D])).then_inc(s_bias[4], 16)
            for c in range(NC):
                def load_x(t, i):
                    sp.dma_start(xrow[:, i, :], x[ds(P * t, P), c * CW:(c + 1) * CW]).then_inc(g_x[i], 16)

                def store_y(t, i):
                    sp.wait_ge(y_ready, START + TT * c + t + 1)
                    sp.dma_start(y1[c, ds(t, 1)].rearrange("a p n -> (a p) n"), yrow[:, i, :]).then_inc(g_out[i], 16)

                for i in range(2):
                    load_x(i, i)
                if c == 0:
                    load_weights(rg, wg)
                with sp.Fori(0, TT // 2 - 1) as g:
                    for i in range(2):
                        store_y(2 * g + i, i)
                        load_x(2 * g + 2 + i, i)
                for i in range(2):
                    store_y(TT - 2 + i, i)

            graph_over(sp)
            sp.dma_start(qf[:, 0:M], orf).then_inc(a_orf, 16)
            with sp.Fori(0, KT) as j:
                for i, w in enumerate((wk, wv, wq)):
                    sp.wait_ge(a_w, START + 3 * j + i)
                    sp.dma_start(hraw[:, :, :], w[ds(j, 1)].rearrange("a p k n -> (a p) k n")).then_inc(a_raw, 16)

            attention_over(sp)
            for c in range(NC):
                for i in range(2):
                    if c:
                        sp.wait_ge(ro.free, TT * c + 1 + i)
                    sp.dma_start(yrow[:, i, :], y1[c, i]).then_inc(o_y[i], 16)
                if c == 0:
                    load_weights(ro, wo)
                with sp.Fori(1, TT // 2) as g:
                    for i in range(2):
                        sp.wait_ge(ro.free, TT * c + 2 * g + 1 + i)
                        sp.dma_start(yrow[:, i, :], y1[c, ds(2 * g + i, 1)].rearrange("a p n -> (a p) n")).then_inc(o_y[i], 16)
            sp.wait_ge(ro.low, NC * TT + 1)
            sp.wait_ge(ro.high, NC * TT + 2)
            sp.wait_ge(ro.free, NC * TT + 2)
            sp.dma_start(gw[:, :, :], gate_w).then_inc(s_bias[5], 16)
            sp.dma_start(gb[:, :], gate_b.broadcast_to([P, E])).then_inc(s_bias[6], 16)

            def load_expert(e, par):
                for k in range(KT):
                    src = expert_w[e, k] if isinstance(e, int) else expert_w[ds(e, 1), k].rearrange("a p n -> (a p) n")
                    sp.dma_start(mraw[par][:, k, :], src).then_inc(mw_raw[k], 16)

            def load_bias(e):
                sp.dma_start(ebb[:, :], expert_b[ds(e, 1)].broadcast_to([P, D])).then_inc(eb_ready, 16)

            load_expert(0, 0)
            load_bias(0)
            for t in range(TT):
                sp.wait_ge(s_xhat, t + 1)
                for c in range(NC):
                    sp.dma_start(x2n_half[c][t * P:(t + 1) * P, :],
                                 xhat[:, t % 2, c * CW:(c + 1) * CW]).then_inc(x2n_stored[t % 2], 16)
            load_expert(1, 1)

            def store_tile(T, e, last):
                for c in range(NC):
                    sp.wait_ge(y_copied[c], T + 3)
                    sp.dma_start(slot_y[ds(T * P, P), c * CW:(c + 1) * CW],
                                 ybuf[:, c, :]).then_inc((z_stored if last else y_stored)[c], 16)

            def expert(e, par, last):
                more, begin = tiles(sp, e)
                with sp.Fori(0, more) as i:
                    store_tile(tile_of(begin + i), e, last)
                T = tile_of(begin + more)
                if not (isinstance(e, int) and e >= E - 2):
                    sp.wait_ge(prod_done, T + 1)
                    load_expert(e + 2, par)
                store_tile(T, e, last)
                if not last:
                    load_bias(e + 1)

            sp.wait_ge(slots_filled, 16 * -(-MAXT * P // NP))
            sp.wait_ge(s_cnti, 1)
            experts(sp, expert)

            for t in range(TT):
                n = LAST if t == TT - 1 else P
                sp.wait_ge(comb_b, t + 1)
                sp.dma_start(out[t * P:t * P + n, :], x2[0:n, t, :]).then_inc(s_out, 16)
            sp.wait_ge(s_out, 16 * TT)

        @block.gpsimd
        def _(pool):
            g = nc.gpsimd
            g.memset(ident[:, :], 0.0).then_inc(s_const, 1)
            g.memset(diag[:, :], 0.0).then_inc(s_const, 1)
            pool.wait_ge(s_const, 2)
            g.affine_select(out=ident[:, :], in_=ident[:, :], compare_op=ALU.not_equal, fill=1.0, base=0,
                            pattern=[[-1, P]], channel_multiplier=1).then_inc(s_cst2, 1)
            g.affine_select(out=diag[:, NP - P:NP], in_=diag[:, NP - P:NP], compare_op=ALU.not_equal, fill=1.0,
                            base=0, pattern=[[-1, P]], channel_multiplier=1).then_inc(s_cst2, 1)
            g.iota(iota[:, :], [[1, NP]], base=0, channel_multiplier=0,
                   allow_small_or_imprecise_dtypes=True).then_inc(s_cst2, 1)
            g.iota(blo[:, :], [[P, TT]], base=0, channel_multiplier=0,
                   allow_small_or_imprecise_dtypes=True).then_inc(s_cst2, 1)
            g.iota(bhi[:, :], [[P, TT]], base=P - 1, channel_multiplier=0,
                   allow_small_or_imprecise_dtypes=True).then_inc(s_cst2, 1)
            g.iota(up[:, :], [[0, 1]], base=1, channel_multiplier=1,
                   allow_small_or_imprecise_dtypes=True).then_inc(s_cst2, 1)
            g.iota(down[:, :], [[0, 1]], base=PAIRS, channel_multiplier=-1,
                   allow_small_or_imprecise_dtypes=True).then_inc(s_cst2, 1)
            g.memset(ones[:, :], 1.0).then_inc(s_cst2, 1)
            g.memset(mhalf[:, :], -0.5).then_inc(s_cst2, 1)
            g.memset(degacc[:, :], 0.0).then_inc(s_pchain, 1)
            pool.sem_inc(oh_free, 4)
            pool.sem_inc(at_evac, 2)
            pool.sem_inc(ax_evac, 2)
            for r in (rg, ro):
                pool.sem_inc(r.free, 2)
            pool.sem_inc(proj_done, 6)
            pool.sem_inc(qf_ready, 3)
            pool.sem_inc(exp_done, 2)
            pool.sem_inc(aux_evac, 2)

            for signal in (a_w, t_done, s_done, sq_ready, phi_done, kv_done, aux_done, kv_evac, g_c, y_ready, *g_out,
                           mt_trans, *y_stored, *z_stored):
                pool.sem_inc(signal, START)
            for c in range(NC):
                pool.sem_inc(y_copied[c], 2)

            pool.wait_ge(s_ext, 1)
            g.partition_all_reduce(extr[:, :], ext[:, :], PAIRS, RMAX).then_inc(s_extr, 1)

            with pool.Fori(0, TT) as b:
                pool.wait_ge(at_evac, b + 3)
                pool.wait_ge(s_pchain, b + 1)
                g.tensor_tensor(degacc[:, :], degacc[:, :], AT[:, ds(b, 1), :].rearrange("p a n -> p (a n)"), ALU.add).then_inc(s_pchain, 1)
            pool.wait_ge(s_pchain, TT + 1)
            pool.wait_ge(ln_a, 3 * TT)
            g.tensor_scalar(varx[:, :], ssq[:, :], 1.0 / D, EPS_LN, ALU.mult, ALU.add).then_inc(s_degacc, 1)
            pool.wait_ge(s_degacc, 1)
            g.tensor_tensor(rstd[:, :], varx[:, :], mhalf[:, :], ALU.pow).then_inc(s_rstd, 1)
            pool.wait_ge(s_degcol, TT)
            g.tensor_tensor(dis[:, :], deg[:, :], mhalf[:, :], ALU.pow).then_inc(s_dis, 1)
            pool.wait_ge(s_dis, 1)
            g.memset(degacc[:, :], 0.0).then_inc(s_pchain, 1)
            for t in range(TT):
                pool.wait_ge(s_pchain, TT + 2 + 2 * t)
                g.tensor_scalar(scaled[:, :], AT[:, t, :], dis[:, t:t + 1], None, ALU.mult).then_inc(s_pchain, 1)
                pool.wait_ge(s_pchain, TT + 3 + 2 * t)
                g.tensor_tensor(degacc[:, :], degacc[:, :], scaled[:, :], ALU.add).then_inc(s_pchain, 1)

            def split_weights(r):
                pool.wait_ge(r.wready, KT)
                for k in range(KT):
                    split_slab(r, 1, k)

            def split_slab(r, c, k):
                cp = c % 2 if isinstance(c, int) else c & 1
                pool.wait_ge(r.raw[k % 4], 16 * (2 * c + k // 4 + 1))
                g.tensor_copy(wh[:, ds(cp, 1), k, :].rearrange("p a n -> p (a n)"), raw[:, k % 4, :]).then_inc(r.whigh, 1)
                pool.wait_ge(r.whigh, KT * c + k + 1)
                g.tensor_tensor(wl[:, ds(cp, 1), k, :].rearrange("p a n -> p (a n)"), raw[:, k % 4, :],
                                wh[:, ds(cp, 1), k, :].rearrange("p a n -> p (a n)").bitcast(F32), ALU.subtract).then_inc(r.wready, 1)

            pool.wait_ge(ax_done, KT)
            pool.wait_ge(s_adcol, TT)
            split_weights(rg)

            graph_over(pool)
            g.memset(negr[:, :].bitcast(F32), -1.0).then_inc(a_cst, 1)
            g.memset(vt[:, :, :, DK:DK + 1], 1.0).then_inc(a_cst, 1)
            pool.wait_ge(a_orf, 16)
            g.tensor_copy(orfh[:, :], qf[:, 0:M]).then_inc(a_cst, 1)
            pool.wait_ge(a_cst, 3)
            g.tensor_tensor(orfl[:, :], qf[:, 0:M], orfh[:, :].bitcast(F32), ALU.subtract).then_inc(a_cst, 1)

            def split_head(j, i):
                pool.wait_ge(proj_done, 9 * j + 3 * i)
                pool.wait_ge(a_raw, 16 * (3 * j + i + 1))
                apart(pool)
                g.tensor_copy(hw[:, i, 0], hraw[:, :, :]).then_inc(a_high, 1)
                pool.wait_ge(a_high, 3 * j + i + 1)
                g.tensor_tensor(hw[:, i, 1], hraw[:, :, :], hw[:, i, 0].bitcast(F32), ALU.subtract).then_inc(a_w, 1)

            for i in range(3):
                split_head(0, i)

            with pool.Fori(0, KT - 1) as j:
                for i in range(3):
                    split_head(j + 1, i)

            attention_over(pool)
            split_weights(ro)
            pool.wait_ge(s_mean, TT)
            g.tensor_scalar(varx[:, :], aggr[:, :, 1:2].rearrange("p t a -> p (t a)"), EPS_LN, None, ALU.add).then_inc(s_rstd2, 1)
            pool.wait_ge(s_rstd2, 1)
            g.tensor_tensor(rstd[:, :], varx[:, :], mhalf[:, :], ALU.pow).then_inc(s_rstd2, 1)
            g.iota(iota8[:, :, :], [[0, TT], [1, E]], base=0, channel_multiplier=0,
                   allow_small_or_imprecise_dtypes=True).then_inc(s_route_const, 1)
            g.iota(thr[:, :, :], [[0, E], [P, TT]], base=P, channel_multiplier=0,
                   allow_small_or_imprecise_dtypes=True).then_inc(s_route_const, 1)
            g.iota(token[:, :], [[P, TT]], base=0, channel_multiplier=1,
                   allow_small_or_imprecise_dtypes=True).then_inc(s_route_const, 1)
            g.memset(upper[:, :], 1.0).then_inc(s_route_const, 1)
            g.iota(nums[:, :], [[1, P]], base=0, channel_multiplier=0,
                   allow_small_or_imprecise_dtypes=True).then_inc(s_route_const, 1)
            g.iota(starts[:, :], [[P, MAXT]], base=0, channel_multiplier=0,
                   allow_small_or_imprecise_dtypes=True).then_inc(s_route_const, 1)
            pool.wait_ge(s_route_const, 6)
            g.affine_select(out=upper[:, :], in_=upper[:, :], compare_op=ALU.is_gt, fill=0.0, base=0,
                            pattern=[[1, P]], channel_multiplier=-1).then_inc(s_route_const, 1)

            for k in range(KT):
                pool.wait_ge(mw_high, k + 1)
                g.tensor_tensor(mwl0[:, k, :], mraw[0][:, k, :], mwh0[:, k, :].bitcast(F32),
                                ALU.subtract).then_inc(mw_ready, 1)

            def gather_tile(T):
                for c in range(NC):
                    pool.wait_ge(mt_trans, START + 2 * T - 1 + c if c else START + 2 * T - 1)
                    apart(pool)
                    g.tensor_copy(here[:, c:c + 1], slots[:, ds(T, 1)]).then_inc(here_ready, 1)
                    pool.wait_ge(here_ready, 2 * T + c + 1)
                    apart(pool)
                    g.indirect_dma_start(xg[:, c, :], None, x2n_half[c][:, :],
                                         bass.IndirectOffsetOnAxis(ap=here[:, c:c + 1], axis=0)).then_inc(xg_ready[c], 16)

            pool.wait_ge(slots_ready, 1)
            pool.wait_ge(s_cnti, 1)
            for i in range(2):
                pool.wait_ge(x2n_stored[i], 16 * NC * TT // 2)
            for c in range(NC):
                g.tensor_copy(here[:, c:c + 1], slots[:, 0:1]).then_inc(here_ready, 1)
            pool.wait_ge(here_ready, 2)
            for c in range(NC):
                g.indirect_dma_start(xg[:, c, :], None, x2n_half[c][:, :],
                                     bass.IndirectOffsetOnAxis(ap=here[:, c:c + 1], axis=0)).then_inc(xg_ready[c], 16)
            more, begin = tiles(pool, E - 1)
            with pool.Fori(0, begin + more + 1) as T:
                gather_tile(tile_of(T + 1))
            for c in range(NC):
                pool.wait_ge(y_stored[c], START + 16 * begin)
                apart(pool)

            def gather_results(t, i, at, done):
                n = LAST if t == TT - 1 else P
                g.indirect_dma_start(gathered[0:n, at, :], None, slot_y[:, :],
                                     bass.IndirectOffsetOnAxis(ap=pos[0:n, i, t:t + 1], axis=0)).then_inc(done, 16)

            for t in range(TT):
                gather_results(t, 0, t, a_gathered)
            pool.wait_ge(s_pos, 1)
            for c in range(NC):
                pool.wait_ge(z_stored[c], START + 16 + 16 * more)
                apart(pool)
            for t in range(TT):
                if t >= 6:
                    pool.wait_ge(comb_b, t - 5)
                gather_results(t, 1, TT + t % 6, b_gathered[t // 2])

        @block.scalar
        def _(act):
            a = nc.scalar
            for b in range(TT):
                act.wait_ge(s_x[b], 16)
                act.wait_ge(ln_a, 3 * b)
                a.activation(junk[:, :], xn[:, b, :], ACT.Identity, accum_out=sums[:, b:b + 1]).then_inc(ln_a, 1)
                act.wait_ge(ln_a, 3 * b + 1)
                a.mul(negmean[:, b:b + 1], sums[:, b:b + 1], -1.0 / D).then_inc(ln_a, 1)
                act.wait_ge(ln_a, 3 * b + 2)
                a.activation(junk[:, :], xn[:, b, :], ACT.Square, bias=negmean[:, b:b + 1],
                             accum_out=ssq[:, b:b + 1]).then_inc(ln_a, 1)
                act.wait_ge(at_done, b + 1)
                s = 1536 * (b % 2)
                a.activation(AT[:, b, :], PB[:, s:s + NP], ACT.Copy).then_inc(at_evac, 1)

            with act.Fori(0, KT // 2) as j2:
                for p in range(2):
                    j = 2 * j2
                    act.wait_ge(ax_done, j + p + 1)
                    a.activation(axT[:, ds(j + p, 1), :].rearrange("p a n -> p (a n)"), PB[:, 1536 * p:1536 * p + NP],
                                 ACT.Copy).then_inc(ax_evac, 1)

            def highs(r, src):
                a.activation(sth[:, 0], src[:, :, 0:P], ACT.Copy).then_inc(r.high, 1)
                for k in range(KT):
                    act.wait_ge(r.raw[k % 4], 16 * (k // 4 + 1))
                    a.activation(wh[:, 0, k, :], raw[:, k % 4, :], ACT.Copy).then_inc(r.whigh, 1)
                a.activation(sth[:, 1], src[:, :, P:2 * P], ACT.Copy).then_inc(r.high, 1)
                with act.Fori(0, r.chunks) as c:
                    with act.Fori(0, TT // 2 - 1) as g:
                        for p in range(2):
                            act.wait_ge(r.done, TT * c + 2 * g + p + 1)
                            a.activation(sth[:, p], src[:, :, ds(P * (2 * g + 2 + p), P)], ACT.Copy).then_inc(r.high, 1)
                    for p in range(2):
                        act.wait_ge(r.done, TT * c + TT - 1 + p)
                        a.activation(sth[:, p], src[:, :, p * P:(p + 1) * P], ACT.Copy).then_inc(r.high, 1)

            act.wait_ge(ax_evac, KT + 2)
            act.wait_ge(s_adcol, TT)
            highs(rg, axT)

            for i in range(2 * TT):
                t, k0 = i // 2, 4 * (i % 2)
                act.wait_ge(xt_done, i + 1)
                if i == 0:
                    graph_over(act)
                a.activation(xh[:, k0:k0 + 4, t * P:(t + 1) * P],
                             bank(i % 4).rearrange("p (k n) -> p k n", k=4), ACT.Copy).then_inc(xt_high, 1)

            act.wait_ge(a_cst, 4)
            act.wait_ge(s_bias[0], 16)
            act.wait_ge(s_bias[1], 16)
            act.wait_ge(s_bias[2], 16)
            act.wait_ge(xt_low, 2 * TT)

            def project(j, i, wi):
                c0, n = CHUNKS[i % 3]
                act.wait_ge(proj_done, 6 + 9 * j + 3 * wi + i % 3 + 1)
                act.wait_ge(t_done, START + 6 * j + i)
                act.wait_ge(sq_ready, START + 6 * j + i)
                act.wait_ge(s_done, START + 6 * j + i)
                apart(act)
                a.activation(qf[:, 0:n], bank(i % 3, n), ACT.Identity,
                             bias=biasT[:, wi, ds(j, 1)]).then_inc(qf_ready, 1)
                act.wait_ge(qf_ready, 3 + 6 * j + i + 1)
                a.activation(sqf[:, 0:n], qf[:, 0:n], ACT.Square, scale=SQ_SCALE).then_inc(sq_ready, 1)
                act.wait_ge(sq_ready, START + 6 * j + i + 1)
                act.wait_ge(phi_done, START + 22 * j + (10 if i >= 3 else 0))
                a.activation(sk[0:64, 0, c0:c0 + n], sqf[0:64, 0:n], ACT.Copy)
                a.activation(sk[64:128, 1, c0:c0 + n], sqf[64:128, 0:n], ACT.Copy).then_inc(s_hi, 1)

            def pair(j, last):
                act.wait_ge(aux_done, START + 12 * j)
                for i in range(3):
                    c0, n = CHUNKS[i]
                    act.wait_ge(proj_done, 6 + 9 * j + 3 + i + 1)
                    apart(act)
                    a.activation(vT[:, c0:c0 + n], bank(i, n), ACT.Identity,
                                 bias=biasT[:, 1, ds(j, 1)]).then_inc(vt_ready, 1)
                for h in range(2):
                    act.wait_ge(kv_done, START + 2 * j + h)
                    act.wait_ge(aux_done, START + 12 * j)
                    for i in range(TT // 2):
                        f = 5 * h + i
                        act.wait_ge(phi_done, START + 22 * j + f + 1)
                        a.activation(kphi[:, 2 * i:2 * i + 2, :], bank(3 + f % 2).rearrange("p (t m) -> p t m", t=2),
                                     ACT.Exp, scale=PHI_SCALE).then_inc(exp_done, 1)
                for i in range(3, 6):
                    project(j, i, 2)
                for h in range(2):
                    act.wait_ge(aux_done, START + 12 * j + 4 + 2 * h)
                    for i in range(6):
                        f = 10 + 6 * h + i
                        c0, n = CHUNKS[i // 2]
                        act.wait_ge(phi_done, START + 22 * j + f + 1)
                        a.activation(qphi[:, i % 2, c0:c0 + n], bank(3 + f % 2, n), ACT.Exp,
                                     scale=PHI_SCALE).then_inc(exp_done, 1)
                if not last:
                    for i in range(3):
                        project(j + 1, i, 0)

            for i in range(3):
                project(0, i, 0)
            pairs(act, pair)

            attention_over(act)
            highs(ro, attnT)

            def high(e, k, par):
                act.wait_ge(mw_raw[k], 16 * (e + 1))
                if not isinstance(e, int):
                    apart(act)
                a.activation(mwh[par][:, k, :], mraw[par][:, k, :], ACT.Copy).then_inc(mw_high, 1)

            for i in range(2 * TT):
                t, k0 = i // 2, 4 * (i % 2)
                act.wait_ge(x2t_done, i + 1)
                if t >= 2:
                    act.wait_ge(lg_done, t - 1)
                a.activation(x2T[:, t % 2, k0:k0 + 4, :],
                             bank(i % 4).rearrange("p (k n) -> p k n", k=4), ACT.Copy).then_inc(x2t_evac, 1)
                if i % 2 and t >= TT - KT:
                    high(0, t - (TT - KT), 0)

            act.wait_ge(s_gd, 1)
            a.activation(gd[:, 1, :], gd[:, 0, :], ACT.Exp).then_inc(s_ge, 1)

            def prepare(T, h):
                act.wait_ge(mt_trans, START + 2 * T + h + 1)
                if not isinstance(T, int):
                    apart(act)
                a.activation(mth[:, 4 * h:4 * h + 4, :], bank(4 + h).rearrange("p (k n) -> p k n", k=4),
                             ACT.Copy).then_inc(mt_high, 1)

            def expert(e, par, last):
                more, begin = tiles(act, e)
                with act.Fori(0, more) as i:
                    for h in range(2):
                        prepare(begin + i + 1, h)
                for h in range(2):
                    prepare(begin + more + 1, h)
                    if not last:
                        for k in range(4 * h, 4 * h + 4):
                            high(e + 1, k, 1 - par)

            act.wait_ge(s_cnti, 1)
            for h in range(2):
                prepare(0, h)
            experts(act, expert)

        @block.vector
        def _(dve):
            v = nc.vector
            chain = [0]

            def link(ins):
                chain[0] += 1
                ins.then_inc(s_dchain, 1)
                dve.wait_ge(s_dchain, chain[0])

            dve.wait_ge(s_edges[0], 16)
            link(v.tensor_copy(dpf[:, :], dpi[:, :]))
            dve.wait_ge(s_cst2, 9)
            dve.wait_ge(s_edges[1], 16)
            dve.wait_ge(s_edges[2], 16)
            link(v.tensor_copy(sc[:, :], sci[:, :]))
            link(v.tensor_copy(dc[:, :], dci[:, :]))
            link(v.tensor_reduce(dmin[:, :], dpf[:, :], AX.X, ALU.min))
            link(v.tensor_reduce(dmax[:, :], dpf[:, :], AX.X, ALU.max))
            link(v.tensor_scalar(rel[:, :], bhi[:, :], dmin[:, :], None, ALU.is_ge))
            link(v.scalar_tensor_tensor(out=rel[:, :], in0=blo[:, :], scalar=dmax[:, :], in1=rel[:, :],
                                        op0=ALU.is_le, op1=ALU.mult))
            link(v.tensor_scalar(ext[:, 0:TT], rel[:, :], up[:, :], None, ALU.mult))
            v.tensor_scalar(ext[:, TT:2 * TT], rel[:, :], down[:, :], None, ALU.mult).then_inc(s_ext, 1)
            dve.wait_ge(s_extr, 1)
            link(v.tensor_scalar(rng[:, 0, :], extr[0:1, TT:2 * TT], -1.0, float(PAIRS), ALU.mult, ALU.add))
            link(v.tensor_tensor(rng[:, 1, :], extr[0:1, 0:TT], rng[:, 0, :], ALU.subtract))
            link(v.tensor_scalar(rng[:, 0, :], rng[:, 0, :], float(PAIRS - 1), None, ALU.min))
            link(v.tensor_scalar(rng[:, 1, :], rng[:, 1, :], 1.0, None, ALU.max))
            link(v.memset(rng[:, 3, :], 0.0))
            link(v.tensor_tensor_scan(rng[:, 2, :], rng[:, 1, :], rng[:, 3, :], 0.0, ALU.add, ALU.add))
            link(v.tensor_tensor(rng[:, 3, :], rng[:, 2, :], rng[:, 1, :], ALU.subtract))
            v.tensor_copy(rngi[:, :, :], rng[:, :, :]).then_inc(s_rng, 1)
            dve.wait_ge(s_rng, 1)

            with dve.Fori(0, TT) as b:
                first = dve.value_load(rngi[0:1, 0, ds(b, 1)], min_val=0, max_val=PAIRS - 1)
                count = dve.value_load(rngi[0:1, 1, ds(b, 1)], min_val=1, max_val=PAIRS)
                begin = dve.value_load(rngi[0:1, 3, ds(b, 1)], min_val=0, max_val=PAIRS * TT)
                with dve.Fori(0, count) as i:
                    at = nc.s_assert_within(first + i, 0, PAIRS - 1, skip_runtime_bounds_check_because="first + count is at most PAIRS")
                    side = dve.snap((begin + i) & 1)
                    for p in range(2):
                        col = 2 * at + p
                        dve.wait_ge(oh_free, 2 * (begin + i) + p + 1)
                        v.tensor_scalar(ohd[:, ds(2 * side + p, 1), :].rearrange("p a n -> p (a n)"),
                                        iota[:, ds(b * P, P)], dc[:, ds(col, 1)], None, ALU.is_equal)
                        v.tensor_scalar(ohs[:, ds(2 * side + p, 1), :].rearrange("p a n -> p (a n)"), iota[:, :],
                                        sc[:, ds(col, 1)], None, ALU.is_equal).then_inc(oh_ready, 1)

            dve.wait_ge(s_deg, 1)
            for t in range(TT):
                dve.wait_ge(s_degcol, t)
                v.tensor_tensor_reduce(out=dscr[:, :], in0=PB[:, t * P:(t + 1) * P], in1=ident[:, :], scale=1.0,
                                       scalar=0.0, op0=ALU.mult, op1=ALU.add,
                                       accum_out=deg[:, t:t + 1]).then_inc(s_degcol, 1)
            dve.wait_ge(s_rstd, 1)
            for t in range(TT):
                v.tensor_scalar(xn[:, t, :], xn[:, t, :], negmean[:, t:t + 1], rstd[:, t:t + 1], ALU.add,
                                ALU.mult).then_inc(s_xn, 1)
            dve.wait_ge(s_xn, TT)
            dve.wait_ge(s_dis, 1)
            with dve.Fori(0, KT // 2) as j2:
                for p in range(2):
                    j = 2 * j2
                    dve.wait_ge(ax_evac, j + p + 1)
                    for t in range(TT):
                        ins = v.tensor_scalar(xs[:, p, t, :], xn[:, t, ds((j + p) * P, P)], dis[:, t:t + 1], None, ALU.mult)
                    ins.then_inc(xs_ready, 1)
            dve.wait_ge(s_ad, 1)
            for t in range(TT):
                dve.wait_ge(s_adcol, t)
                v.tensor_tensor_reduce(out=dscr[:, :], in0=PB[:, t * P:(t + 1) * P], in1=ident[:, :], scale=1.0,
                                       scalar=0.0, op0=ALU.mult, op1=ALU.add,
                                       accum_out=adis[:, t:t + 1]).then_inc(s_adcol, 1)

            def rows(r, src, finish):
                def lows(T, p, at):
                    dve.wait_ge(r.high, T + 1)
                    v.tensor_tensor(stl[:, p], src[:, :, at], sth[:, p].bitcast(F32), ALU.subtract).then_inc(r.low, 1)

                lows(0, 0, slice(0, P))
                for k in range(KT):
                    dve.wait_ge(r.whigh, k + 1)
                    v.tensor_tensor(wl[:, 0, k, :], raw[:, k % 4, :], wh[:, 0, k, :].bitcast(F32),
                                    ALU.subtract).then_inc(r.wready, 1)
                with dve.Fori(0, r.chunks) as c:
                    with dve.Fori(0, TT // 2 - 1) as g:
                        for p in range(2):
                            T = TT * c + 2 * g + p
                            lows(T + 1, (p + 1) % 2, ds(P * (2 * g + p + 1), P))
                            dve.wait_ge(r.done, T + 1)
                            finish(c, 2 * g + p, p, T, g)
                    for p in range(2):
                        t = TT - 2 + p
                        T = TT * c + t
                        lows(T + 1, (p + 1) % 2, slice((TT - 1) * P, NP) if p == 0 else slice(0, P))
                        dve.wait_ge(r.done, T + 1)
                        finish(c, t, p, T, TT // 2 - 1)

            def finish_graph(c, t, p, T, g):
                dve.wait_ge(g_x[p], 16 * (TT // 2 * c + g + 1))
                dve.wait_ge(g_c, START + T)
                dve.wait_ge(y_ready, START + T)
                v.scalar_tensor_tensor(out=u1[:, :], in0=bgb[:, ds(c * CW, CW)], scalar=adis[:, ds(t, 1)],
                                       in1=bank(6 + p), op0=ALU.mult, op1=ALU.add).then_inc(rg.free, 1)
                dve.wait_ge(rg.free, T + 3)
                v.scalar_tensor_tensor(out=u2[:, :], in0=u1[:, :], scalar=dis[:, ds(t, 1)],
                                       in1=xrow[:, p, :], op0=ALU.mult, op1=ALU.add).then_inc(g_c, 1)
                dve.wait_ge(g_c, START + T + 1)
                dve.wait_ge(g_out[p], START + 16 * (TT // 2 * c + g))
                v.tensor_tensor(yrow[:, p, :], u2[:, :], bob[:, ds(c * CW, CW)], ALU.add).then_inc(y_ready, 1)

            dve.wait_ge(s_bias[3], 16)
            dve.wait_ge(s_bias[4], 16)
            rows(rg, axT, finish_graph)

            for i in range(2 * TT):
                t, k0 = i // 2, 4 * (i % 2)
                dve.wait_ge(xt_high, i + 1)
                if i == 0:
                    graph_over(dve)
                v.tensor_tensor(xl[:, k0:k0 + 4, t * P:(t + 1) * P], bank(i % 4).rearrange("p (k n) -> p k n", k=4),
                                xh[:, k0:k0 + 4, t * P:(t + 1) * P].bitcast(F32), ALU.subtract).then_inc(xt_low, 1)
            dve.wait_ge(a_cst, 4)

            def stack(j, i):
                c0, n = CHUNKS[i % 3]
                dve.wait_ge(qf_ready, 3 + 6 * j + i + 1)
                dve.wait_ge(phi_done, START + 22 * j + (10 if i >= 3 else 0))
                v.tensor_copy(tk[0:64, 0, c0:c0 + n], qf[0:64, 0:n])
                v.tensor_copy(tk[64:128, 1, c0:c0 + n], qf[64:128, 0:n]).then_inc(t_hi, 1)
                dve.wait_ge(t_hi, 6 * j + i + 1)
                v.tensor_tensor(tk[64:128, 0, c0:c0 + n], qf[0:64, 0:n], tk[0:64, 0, c0:c0 + n].bitcast(F32), ALU.subtract)
                v.tensor_tensor(tk[0:64, 1, c0:c0 + n], qf[64:128, 0:n], tk[64:128, 1, c0:c0 + n].bitcast(F32),
                                ALU.subtract).then_inc(t_done, 1)
                dve.wait_ge(s_hi, 6 * j + i + 1)
                v.tensor_tensor(sk[64:128, 0, c0:c0 + n], sqf[0:64, 0:n], sk[0:64, 0, c0:c0 + n].bitcast(F32), ALU.subtract)
                v.tensor_tensor(sk[0:64, 1, c0:c0 + n], sqf[64:128, 0:n], sk[64:128, 1, c0:c0 + n].bitcast(F32),
                                ALU.subtract).then_inc(s_done, 1)

            def pair(j, last):
                dve.wait_ge(kv_done, START + 2 * j)
                for i, (t0, nt) in enumerate(((0, 3), (3, 3), (6, 2), (8, 2))):
                    dve.wait_ge(aux_done, START + 12 * j + i + 1)
                    v.tensor_copy(vt[:, t0:t0 + nt, :, 0:DK],
                                  bank(6 + i % 2, nt * P).rearrange("p (t h d) -> p t h d", t=nt, h=2)).then_inc(aux_evac, 1)
                for h in range(2):
                    for i in range(TT // 2):
                        dve.wait_ge(exp_done, 2 + 22 * j + 5 * h + i + 1)
                        v.tensor_scalar(kphi[:, 2 * i:2 * i + 2, :], kphi[:, 2 * i:2 * i + 2, :], EPS_PHI, None,
                                        ALU.add).then_inc(kph_ready, 1)
                    if h == 1:
                        for i in range(3, 6):
                            stack(j, i)
                    dve.wait_ge(aux_done, START + 12 * j)
                    dve.wait_ge(kv_done, START + 2 * j + h + 1)
                    v.tensor_copy(kvs[:, h, :, :], bank(5, MH * (DK + 1)).rearrange("p (m d) -> p m d", m=MH)).then_inc(kv_evac, 1)
                for h in range(2):
                    for i in range(6):
                        c0, n = CHUNKS[i // 2]
                        dve.wait_ge(exp_done, 2 + 22 * j + 10 + 6 * h + i + 1)
                        v.tensor_scalar(qphi[:, i % 2, c0:c0 + n], qphi[:, i % 2, c0:c0 + n], EPS_PHI, None,
                                        ALU.add).then_inc(qph_ready, 1)
                    for i in range(2):
                        f = 4 + 2 * h + i
                        half = bank(6 + f % 2, 5 * (DK + 1)).rearrange("p (t d) -> p t d", t=5)
                        dve.wait_ge(aux_done, START + 12 * j + f + 1)
                        dve.wait_ge(aux_evac, 2 + 12 * j + f)
                        v.reciprocal(rec[:, :], half[:, :, DK:DK + 1].rearrange("p t a -> p (t a)")).then_inc(rec_done, 1)
                        dve.wait_ge(rec_done, 4 * j + 2 * h + i + 1)
                        v.tensor_tensor(att[:, 5 * i:5 * i + 5, DK * h:DK * h + DK], half[:, :, 0:DK],
                                        rec[:, :].rearrange("p (t a) -> p t a", a=1).broadcast_to([P, 5, DK]),
                                        ALU.mult).then_inc(aux_evac, 1)
                for i, (t0, nt) in enumerate(((0, 3), (3, 3), (6, 2), (8, 2))):
                    if not last and i % 2 == 1:
                        stack(j + 1, i // 2)
                    dve.wait_ge(aux_done, START + 12 * j + 8 + i + 1)
                    v.tensor_copy(attnT[:, ds(j, 1), t0 * P:(t0 + nt) * P].rearrange("p a n -> p (a n)"),
                                  bank(6 + i % 2, nt * P)).then_inc(aux_evac, 1)
                if not last:
                    stack(j + 1, 2)

            for i in range(3):
                stack(0, i)
            pairs(dve, pair)

            def finish_residual(c, t, p, T, g):
                dve.wait_ge(o_y[p], 16 * (TT // 2 * c + g + 1))
                half = x2[:, ds(t, 1), ds(c * CW, CW)].rearrange("p a n -> p (a n)")
                v.tensor_tensor(half, bank(6 + p), yrow[:, p, :], ALU.add).then_inc(ro.free, 1)
                dve.wait_ge(ro.free, T + 3)
                v.bn_stats(stats[:, ds(t, 1), ds(c, 1), :].rearrange("p t c s -> p (t c s)"), half).then_inc(s_stats, 1)

            attention_over(dve)
            rows(ro, attnT, finish_residual)

            dve.wait_ge(ro.free, NC * TT + 2)
            dve.wait_ge(s_stats, NC * TT)
            for t in range(TT):
                v.bn_aggr(aggr[:, t, :], stats[:, t, :, :]).then_inc(s_mean, 1)
            dve.wait_ge(s_mean, TT)
            dve.wait_ge(s_rstd2, 2)
            dve.wait_ge(ro.high, NC * TT + 2)
            dve.wait_ge(ro.low, NC * TT + 1)
            for t in range(TT):
                if t >= 2:
                    dve.wait_ge(x2t_done, 2 * (t - 1))
                    dve.wait_ge(x2n_stored[t % 2], 16 * NC * (t // 2))
                v.tensor_scalar(xhat[:, t % 2, :], x2[:, t, :], aggr[:, t, 0:1], rstd[:, t:t + 1], ALU.subtract,
                                ALU.mult).then_inc(s_xhat, 1)

            def spread(col):
                return col.rearrange("p (t a) -> p t a", a=1).broadcast_to([P, TT, E])

            dve.wait_ge(s_bias[6], 16)
            dve.wait_ge(lg_done, TT)
            link(v.tensor_tensor(lg[:, :, :], bank(6, TT * E).rearrange("p (t e) -> p t e", t=TT),
                                 gb[:, :].rearrange("p (a e) -> p a e", a=1).broadcast_to([P, TT, E]), ALU.add))
            for t in range(TT):
                v.max(mx[:, t, :], lg[:, t, :]).then_inc(s_dchain, 1)
            chain[0] += TT
            for t in range(TT):
                dve.wait_ge(s_dchain, chain[0] - TT + t + 1)
                v.max_index(ix[:, t, :], mx[:, t, :], lg[:, t, :]).then_inc(s_dchain, 1)
            chain[0] += TT
            dve.wait_ge(s_dchain, chain[0])
            v.tensor_tensor(gd[:, 0, :], mx[:, :, 1:2].rearrange("p t a -> p (t a)"),
                            mx[:, :, 0:1].rearrange("p t a -> p (t a)"), ALU.subtract).then_inc(s_gd, 1)
            link(v.tensor_copy(ixf[:, :, :], ix[:, :, :]))
            one, two = (ixf[:, :, i:i + 1].rearrange("p t a -> p (t a)") for i in range(2))
            v.tensor_tensor(ab[:, 0, :], one, two, ALU.min).then_inc(s_dchain, 1)
            v.tensor_tensor(ab[:, 1, :], one, two, ALU.max).then_inc(s_dchain, 1)
            chain[0] += 2
            dve.wait_ge(s_dchain, chain[0])
            dve.wait_ge(s_route_const, 7)
            v.tensor_tensor(oneh[:, 0], iota8[:, :, :], spread(ab[:, 0, :]), ALU.is_equal).then_inc(s_dchain, 1)
            v.tensor_tensor(oneh[:, 1], iota8[:, :, :], spread(ab[:, 1, :]), ALU.is_equal).then_inc(s_dchain, 1)
            chain[0] += 2
            dve.wait_ge(s_dchain, chain[0])
            v.tensor_tensor(both[:, :, :], oneh[:, 0], oneh[:, 1], ALU.add).then_inc(s_both, 1)
            dve.wait_ge(ranks_done, 1)
            rank = bank(0, TT * E).rearrange("p (t e) -> p t e", t=TT)
            link(v.tensor_copy(tot[:, :, :], bank(1, TT * E).rearrange("p (t e) -> p t e", t=TT)))
            link(v.tensor_reduce(cnt[:, 0, :], tot[:, :, :].rearrange("p t e -> p e t"), AX.X, ALU.add))
            link(v.tensor_tensor(over[:, :, :], cnt[:, 0, :].rearrange("p (e a) -> p e a", a=1).broadcast_to([P, E, TT]),
                                 thr[:, :, :], ALU.is_gt))
            link(v.tensor_reduce(cnt[:, 1, :], over[:, :, :], AX.X, ALU.add))
            link(v.tensor_scalar(cnt[:, 1, :], cnt[:, 1, :], 1.0, 2.0, ALU.add, ALU.max))
            link(v.memset(cnt[:, 3, :], 0.0))
            link(v.tensor_tensor_scan(cnt[:, 2, :], cnt[:, 1, :], cnt[:, 3, :], 0.0, ALU.add, ALU.add))
            link(v.tensor_tensor(cnt[:, 3, :], cnt[:, 2, :], cnt[:, 1, :], ALU.subtract))
            link(v.tensor_scalar(cnt[:, 0, :], cnt[:, 1, :], -1.0, None, ALU.add))
            v.tensor_copy(cnti[:, :, :], cnt[0:1, :, :]).then_inc(s_cnti, 1)
            link(v.tensor_scalar(carry[:, 0, :], cnt[:, 3, :], float(P), None, ALU.mult))
            for t in range(TT - 1):
                link(v.tensor_tensor(carry[:, t + 1, :], carry[:, t, :], tot[:, t, :], ALU.add))
            link(v.tensor_tensor(carry[:, :, :], rank, carry[:, :, :], ALU.add))
            for i in range(2):
                link(v.tensor_tensor(both[:, :, :], oneh[:, i], carry[:, :, :], ALU.mult))
                link(v.tensor_reduce(posf[:, i, :], both[:, :, :], AX.X, ALU.add))
            v.tensor_copy(pos[:, :, :], posf[:, :, :]).then_inc(s_pos, 1)
            flat = posf[:, :, :].rearrange("p i t -> p (i t)")

            def along(col, n):
                return col.rearrange("p (s a) -> p s a", a=1).broadcast_to([P, 2 * TT, n])

            def across(row, n):
                return row.rearrange("p (a n) -> p a n", a=1).broadcast_to([P, 2 * TT, n])

            link(v.tensor_tensor(hota[:, :, :], across(starts[:, :], MAXT), along(flat, MAXT), ALU.is_le))
            link(v.tensor_reduce(posa[:, :], hota[:, :, :], AX.X, ALU.add))
            link(v.tensor_scalar(posa[:, :], posa[:, :], -1.0, None, ALU.add))
            link(v.scalar_tensor_tensor(out=posr[:, :], in0=posa[:, :], scalar=-float(P), in1=flat, op0=ALU.mult, op1=ALU.add))
            v.tensor_tensor(hotr[:, :, :], across(nums[:, :], P), along(posr[:, :], P), ALU.is_equal).then_inc(slot_hot, 1)
            link(v.tensor_tensor(hota[:, :, :], across(nums[:, 0:MAXT], MAXT), along(posa[:, :], MAXT), ALU.is_equal))
            for i in range(2):
                v.tensor_tensor(hott[:, i * TT:(i + 1) * TT, :], hota[:, i * TT:(i + 1) * TT, :],
                                token[:, :].rearrange("p (t a) -> p t a", a=1).broadcast_to([P, TT, MAXT]),
                                ALU.mult).then_inc(slot_hot, 1)
            def prepare(T, h):
                dve.wait_ge(mt_high, 2 * T + h + 1)
                v.tensor_tensor(mtl[:, 4 * h:4 * h + 4, :], bank(4 + h).rearrange("p (k n) -> p k n", k=4),
                                mth[:, 4 * h:4 * h + 4, :].bitcast(F32), ALU.subtract).then_inc(mt_low, 1)

            def copy_out(T, e, i, begin, last):
                for c in range(NC):
                    dve.wait_ge(prod_done, T + 1)
                    dve.wait_ge(eb_ready, 16 * (e + 1))
                    if last:
                        dve.wait_ge(y_stored[c], START + 16 * begin)
                        dve.wait_ge(z_stored[c], START + 16 * i)
                    else:
                        dve.wait_ge(y_stored[c], START + 16 * T)
                    v.tensor_tensor(ybuf[:, c, :], PB[:, ds((T & 1) * D + c * CW, CW)], ebb[:, c * CW:(c + 1) * CW],
                                    ALU.add).then_inc(y_copied[c], 1)

            def expert(e, par, last):
                more, begin = tiles(dve, e)
                with dve.Fori(0, more) as i:
                    for h in range(2):
                        prepare(begin + i + 1, h)
                    copy_out(begin + i, e, i, begin, last)
                for h in range(2):
                    prepare(begin + more + 1, h)
                    if not last:
                        for k in range(4 * h, 4 * h + 4):
                            dve.wait_ge(mw_high, KT * (e + 1) + k + 1)
                            v.tensor_tensor(mwl[1 - par][:, k, :], mraw[1 - par][:, k, :],
                                            mwh[1 - par][:, k, :].bitcast(F32), ALU.subtract).then_inc(mw_ready, 1)
                copy_out(begin + more, e, more, begin, last)

            dve.wait_ge(slots_done, 1)
            v.tensor_copy(slots[:, :], bank(2, MAXT)).then_inc(slots_ready, 1)
            dve.wait_ge(s_ge, 1)
            link(v.tensor_scalar(gd[:, 3, :], gd[:, 1, :], 1.0, None, ALU.add))
            link(v.reciprocal(gd[:, 2, :], gd[:, 3, :]))
            link(v.tensor_tensor(gd[:, 3, :], gd[:, 1, :], gd[:, 2, :], ALU.mult))
            link(v.tensor_tensor(sel[:, 0, :], one, two, ALU.is_lt))
            link(v.tensor_tensor(sel[:, 1, :], two, one, ALU.is_lt))
            for i in range(2):
                link(v.tensor_tensor(gab[:, 1, i, :], sel[:, i, :], gd[:, 2, :], ALU.mult))
                link(v.tensor_tensor(gab[:, 2, i, :], sel[:, 1 - i, :], gd[:, 3, :], ALU.mult))
                link(v.tensor_tensor(gab[:, 0, i, :], gab[:, 1, i, :], gab[:, 2, i, :], ALU.add))
            dve.wait_ge(s_cnti, 1)
            for h in range(2):
                prepare(0, h)
            experts(dve, expert)

            def combine(t, i, at, done):
                n = LAST if t == TT - 1 else P
                v.scalar_tensor_tensor(out=x2[0:n, t, :], in0=gathered[0:n, at, :], scalar=gab[0:n, 0, i, t:t + 1],
                                       in1=x2[0:n, t, :], op0=ALU.mult, op1=ALU.add).then_inc(done, 1)

            dve.wait_ge(a_gathered, 16 * TT)
            for t in range(TT):
                combine(t, 0, t, comb_a)
            for t in range(TT):
                dve.wait_ge(comb_a, t + 1)
                dve.wait_ge(b_gathered[t // 2], 32)
                combine(t, 1, TT + t % 6, comb_b)

        @block.tensor
        def _(pe):
            mm = nc.tensor.matmul
            pe.wait_ge(s_rng, 1)
            pe.wait_ge(s_cst2, 9)
            with pe.Fori(0, TT // 2) as b2:
                for s in range(2):
                    b = 2 * b2 + s
                    first = pe.value_load(rngi[0:1, 0, ds(b, 1)], min_val=0, max_val=PAIRS - 1)
                    count = pe.value_load(rngi[0:1, 1, ds(b, 1)], min_val=1, max_val=PAIRS)
                    begin = pe.value_load(rngi[0:1, 3, ds(b, 1)], min_val=0, max_val=PAIRS * TT)
                    pe.wait_ge(at_evac, b + 1)
                    for c0, n in CHUNKS:
                        mm(PB[:, 1536 * s + c0:1536 * s + c0 + n], diag[:, NP - P:NP],
                           diag[:, ds(NP - P - P * b + c0, n)], start=True, stop=False, skip_group_check=True)
                    with pe.Fori(0, count) as i:
                        side = pe.snap((begin + i) & 1)
                        for p in range(2):
                            pe.wait_ge(oh_ready, 2 * (begin + i) + p + 1)
                            for c0, n in CHUNKS:
                                ins = mm(PB[:, 1536 * s + c0:1536 * s + c0 + n],
                                         ohd[:, ds(2 * side + p, 1), :].rearrange("p a n -> p (a n)"),
                                         ohs[:, ds(2 * side + p, 1), c0:c0 + n].rearrange("p a n -> p (a n)"),
                                         start=False, stop=False, skip_group_check=True)
                            ins.then_inc(oh_free, 1)
                    for c0, n in CHUNKS:
                        ins = mm(PB[:, 1536 * s + c0:1536 * s + c0 + 2], diag[:, NP - P:NP], diag[:, 0:2],
                                 start=False, stop=True, skip_group_check=True)
                    ins.then_inc(at_done, 1)

            pe.wait_ge(s_pchain, TT + 1)
            pe.wait_ge(at_evac, TT + 2)
            for c0, n in CHUNKS:
                ins = mm(PB[:, c0:c0 + n], ones[:, :], degacc[:, c0:c0 + n], start=True, stop=True)
            ins.then_inc(s_deg, 1)
            with pe.Fori(0, KT // 2) as j2:
                for s in range(2):
                    j = 2 * j2
                    pe.wait_ge(xs_ready, j + s + 1)
                    pe.wait_ge(ax_evac, j + s + 1)
                    for c0, n in CHUNKS:
                        for t in range(TT):
                            ins = mm(PB[:, 1536 * s + c0:1536 * s + c0 + n], xs[:, s, t, :], AT[:, t, c0:c0 + n],
                                     start=(t == 0), stop=(t == TT - 1))
                    ins.then_inc(ax_done, 1)
            pe.wait_ge(s_pchain, 3 * TT + 2)
            pe.wait_ge(ax_evac, KT + 2)
            for c0, n in CHUNKS:
                ins = mm(PB[:, c0:c0 + n], ones[:, :], degacc[:, c0:c0 + n], start=True, stop=True)
            ins.then_inc(s_ad, 1)

            def rows(r):
                with pe.Fori(0, r.chunks) as c:
                    cp = c & 1
                    with pe.Fori(0, TT // 2) as g:
                        for p in range(2):
                            T = TT * c + 2 * g + p
                            pe.wait_ge(r.low, T + 1)
                            pe.wait_ge(r.free, T + 1)
                            for k in range(KT):
                                pe.wait_ge(r.wready, KT * c + k + 1)
                                high = wh[:, ds(cp, 1), k, :].rearrange("p a n -> p (a n)")
                                lowr = wl[:, ds(cp, 1), k, :].rearrange("p a n -> p (a n)")
                                mm(bank(6 + p), sth[:, p, k, :], high, start=(k == 0), stop=False)
                                mm(bank(6 + p), sth[:, p, k, :], lowr, start=False, stop=False)
                                ins = mm(bank(6 + p), stl[:, p, k, :], high, start=False, stop=(k == KT - 1))
                            ins.then_inc(r.done, 1)

            rows(rg)

            for i in range(2 * TT):
                t = i // 2
                if i >= 4:
                    pe.wait_ge(xt_low, i - 3)
                for q in range(4):
                    k = 4 * (i % 2) + q
                    ins = nc.tensor.transpose(bank(i % 4)[:, q * P:(q + 1) * P], xn[:, t, k * P:(k + 1) * P], ident[:, :])
                ins.then_inc(xt_done, 1)
            pe.wait_ge(xt_low, 2 * TT)
            pe.wait_ge(a_cst, 4)

            def project(j, wi, after=None):
                pe.wait_ge(a_w, START + 3 * j + wi + 1)
                for i, (c0, n) in enumerate(CHUNKS):
                    if wi == 0:
                        pe.wait_ge(qf_ready, 6 * j + i + 1)
                    elif wi == 1:
                        pe.wait_ge(qf_ready, 3 + 6 * j + i + 1)
                    else:
                        pe.wait_ge(vt_ready, 3 * j + i + 1)
                    for k in range(KT):
                        mm(bank(i, n), hw[:, wi, 0, k, :], xh[:, k, c0:c0 + n], start=(k == 0), stop=False)
                        mm(bank(i, n), hw[:, wi, 0, k, :], xl[:, k, c0:c0 + n], start=False, stop=False)
                        ins = mm(bank(i, n), hw[:, wi, 1, k, :], xh[:, k, c0:c0 + n], start=False, stop=(k == KT - 1))
                    ins.then_inc(proj_done, 1)
                    if after:
                        after(i)

            def pair(j, last):
                project(j, 1)
                for i, (t0, nt) in enumerate(((0, 3), (3, 3), (6, 2), (8, 2))):
                    pe.wait_ge(aux_evac, 12 * j + i + 1)
                    pe.wait_ge(vt_ready, 3 * j + (1, 2, 2, 3)[i])
                    for q in range(nt):
                        ins = nc.tensor.transpose(bank(6 + i % 2)[:, q * P:(q + 1) * P],
                                                  vT[:, (t0 + q) * P:(t0 + q + 1) * P], ident[:, :])
                    ins.then_inc(aux_done, 1)

                def key_features(h, i):
                    f = 5 * h + i
                    pe.wait_ge(exp_done, 22 * j + f + 1)
                    for q in range(2):
                        at = slice((2 * i + q) * P, (2 * i + q + 1) * P)
                        o = bank(3 + f % 2)[:, q * M:(q + 1) * M]
                        mm(o, tk[:, h, at], orfh[:, :], start=True, stop=False)
                        mm(o, tk[:, h, at], orfl[:, :], start=False, stop=False)
                        ins = mm(o, sk[:, h, at], negr[:, :], start=False, stop=True)
                    ins.then_inc(phi_done, 1)

                def key_values(h):
                    pe.wait_ge(kv_evac, START + 2 * j + h)
                    pe.wait_ge(kph_ready, 10 * j + 5 * h + 5)
                    pe.wait_ge(aux_evac, 2 + 12 * j + 4)
                    for m in range(MH):
                        for t in range(TT):
                            n = LAST if t == TT - 1 else P
                            ins = mm(bank(5)[:, m * (DK + 1):(m + 1) * (DK + 1)], kphi[0:n, t, m * P:(m + 1) * P],
                                     vt[0:n, t, h, :], start=(t == 0), stop=(t == TT - 1))
                    ins.then_inc(kv_done, 1)

                def query_features(h, i):
                    f = 10 + 6 * h + i
                    m = slice(i % 2 * P, i % 2 * P + P)
                    c0, n = CHUNKS[i // 2]
                    pe.wait_ge(exp_done, 22 * j + f + 1)
                    pe.wait_ge(t_done, START + 6 * j + 4 + (i // 2 if h == 0 else 2))
                    pe.wait_ge(s_done, START + 6 * j + 4 + (i // 2 if h == 0 else 2))
                    mm(bank(3 + f % 2, n), orfh[:, m], tk[:, h, c0:c0 + n], start=True, stop=False)
                    mm(bank(3 + f % 2, n), orfl[:, m], tk[:, h, c0:c0 + n], start=False, stop=False)
                    mm(bank(3 + f % 2, n), negr[:, m], sk[:, h, c0:c0 + n], start=False, stop=True).then_inc(phi_done, 1)

                def outputs(h, i):
                    f = 4 + 2 * h + i
                    pe.wait_ge(aux_evac, 12 * j + f + 1)
                    pe.wait_ge(qph_ready, 12 * j + 6 * h + (4 if i == 0 else 6))
                    for q in range(5):
                        t = 5 * i + q
                        for m in range(MH):
                            ins = mm(bank(6 + f % 2)[:, q * (DK + 1):(q + 1) * (DK + 1)],
                                     qphi[:, m, t * P:(t + 1) * P], kvs[:, h, m, :], start=(m == 0), stop=(m == MH - 1))
                    ins.then_inc(aux_done, 1)

                pe.wait_ge(t_done, START + 6 * j + 3)
                pe.wait_ge(s_done, START + 6 * j + 3)
                for i in range(TT // 2):
                    key_features(0, i)
                key_features(1, 0)
                key_values(0)
                for i in range(1, TT // 2):
                    key_features(1, i)
                project(j, 2)
                key_values(1)
                for i in range(6):
                    query_features(0, i)
                query_features(1, 0)
                pe.wait_ge(kv_evac, START + 2 * j + 1)
                outputs(0, 0)
                query_features(1, 1)
                outputs(0, 1)
                for i in range(2, 6):
                    query_features(1, i)
                pe.wait_ge(kv_evac, START + 2 * j + 2)
                outputs(1, 0)
                outputs(1, 1)
                def turn(i):
                    t0, nt = ((0, 3), (3, 3), (6, 2), (8, 2))[i]
                    pe.wait_ge(aux_evac, 12 * j + 8 + i + 1)
                    for q in range(nt):
                        ins = nc.tensor.transpose(bank(6 + i % 2)[:, q * P:(q + 1) * P], att[:, t0 + q, :], ident[:, :])
                    ins.then_inc(aux_done, 1)

                if last:
                    for i in range(4):
                        turn(i)
                else:
                    def turns(i):
                        for q in range(2 * i, min(2 * i + 2, 4)):
                            turn(q)
                    project(j + 1, 0, turns)

            project(0, 0)
            pairs(pe, pair)

            rows(ro)

            def logits(t):
                pe.wait_ge(x2t_evac, 2 * t + 2)
                for k in range(KT):
                    ins = mm(bank(6)[:, t * E:(t + 1) * E], x2T[:, t % 2, k, :], gw[:, k, :], start=(k == 0), stop=(k == KT - 1))
                ins.then_inc(lg_done, 1)

            pe.wait_ge(ro.free, NC * TT + 2)
            pe.wait_ge(s_bias[5], 16)
            for i in range(2 * TT):
                t = i // 2
                pe.wait_ge(s_xhat, t + 1)
                if i >= 4:
                    pe.wait_ge(x2t_evac, i - 3)
                for q in range(4):
                    k = 4 * (i % 2) + q
                    ins = nc.tensor.transpose(bank(i % 4)[:, q * P:(q + 1) * P], xhat[:, t % 2, k * P:(k + 1) * P], ident[:, :])
                ins.then_inc(x2t_done, 1)
                if i % 2 and t >= 1:
                    logits(t - 1)
            logits(TT - 1)
            pe.wait_ge(s_both, 1)
            whole, rest = slice(0, TT - 1), TT - 1
            for b, left in ((0, upper), (1, ones)):
                mm(bank(b, (TT - 1) * E), left[:, :], both[:, whole, :].rearrange("p t e -> p (t e)"), start=True, stop=True)
                ins = mm(bank(b)[:, rest * E:TT * E], left[0:LAST, :], both[0:LAST, rest, :], start=True, stop=True)
            ins.then_inc(ranks_done, 1)

            pe.wait_ge(slot_hot, 3)
            for i in range(2 * TT):
                n = LAST if i % TT == TT - 1 else P
                ins = mm(bank(2, MAXT), hotr[0:n, i, :], hott[0:n, i, :], start=(i == 0), stop=(i == 2 * TT - 1))
            ins.then_inc(slots_done, 1)

            def transposes(T, h):
                pe.wait_ge(xg_ready[h], 16 * (T + 1))
                if not isinstance(T, int):
                    pe.wait_ge(mt_low, 2 * T - 1 + h)
                    apart(pe)
                for q in range(4):
                    ins = nc.tensor.transpose(bank(4 + h)[:, q * P:(q + 1) * P], xg[:, h, q * P:(q + 1) * P], ident[:, :])
                ins.then_inc(mt_trans, 1)

            def tile(T, e, par):
                for c in range(NC):
                    pe.wait_ge(y_copied[c], T + 1)
                apart(pe)
                y = [PB[:, ds((T & 1) * D + c * CW, CW)] for c in range(NC)]
                for h in range(2):
                    pe.wait_ge(mt_low, 2 * T + h + 1)
                    for k in range(4 * h, 4 * h + 4):
                        pe.wait_ge(mw_ready, KT * e + k + 1)
                        for c in range(NC):
                            mm(y[c], mth[:, k, :], mwh[par][:, k, c * CW:(c + 1) * CW], start=(k == 0), stop=False)
                            mm(y[c], mth[:, k, :], mwl[par][:, k, c * CW:(c + 1) * CW], start=False, stop=False)
                        for c in range(NC):
                            ins = mm(y[c], mtl[:, k, :], mwh[par][:, k, c * CW:(c + 1) * CW], start=False, stop=(k == KT - 1))
                    if h == 1:
                        ins.then_inc(prod_done, 1)
                    transposes(T + 1, h)

            def expert(e, par, last):
                more, begin = tiles(pe, e)
                with pe.Fori(0, more + 1) as i:
                    tile(begin + i, e, par)

            pe.wait_ge(s_cnti, 1)
            for h in range(2):
                transposes(0, h)
            experts(pe, expert)



_INS = ["x", "dst_pairs", "src_cols", "dst_cols", "wg", "bg", "wq", "bq", "wk", "bk", "wv", "bv", "wo", "bo", "orf",
        "gate_w", "gate_b", "expert_w", "expert_b"]


def kernel(**inputs):
    import numpy as np
    import concourse.bacc as bacc
    from concourse.bass_utils import run_bass_kernel_spmd

    a = {k: np.asarray(v) for k, v in inputs.items()}

    def chunks(w):
        return w.reshape(KT, P, NC, CW).transpose(2, 0, 1, 3)

    def heads(w):
        return w.T.reshape(KT, P, KT, P).transpose(2, 1, 0, 3)

    def column(b):
        return b.reshape(KT, P).T

    slots = 2 * PAIRS * P
    src = np.pad(a["src"], (0, slots - EDGES), constant_values=-1)
    dst = np.pad(a["dst"], (0, slots - EDGES), mode="edge")
    orfT = a["L0_mix_orf"].T
    arrays = {
        "x": np.pad(a["x"], ((0, NP - N), (0, 0))),
        "dst_pairs": dst.reshape(PAIRS, PAIR),
        "src_cols": src.reshape(2 * PAIRS, P).T,
        "dst_cols": dst.reshape(2 * PAIRS, P).T,
        "wg": chunks(a["L0_gnn_W"].T),
        "bg": a["L0_gnn_b"].reshape(1, D),
        "wq": heads(a["L0_mix_Wq"]), "bq": column(a["L0_mix_bq"]),
        "wk": heads(a["L0_mix_Wk"]), "bk": column(a["L0_mix_bk"]),
        "wv": heads(a["L0_mix_Wv"]), "bv": column(a["L0_mix_bv"]),
        "wo": chunks(a["L0_mix_Wo"].T),
        "bo": a["L0_mix_bo"].reshape(1, D),
        "orf": np.concatenate([orfT, orfT], axis=0),
        "gate_w": a["L0_ffn_gate_w"].T.reshape(KT, P, E).transpose(1, 0, 2),
        "gate_b": a["L0_ffn_gate_b"].reshape(1, E),
        "expert_w": a["L0_ffn_expert_w"].reshape(E, KT, P, D),
        "expert_b": a["L0_ffn_expert_b"],
    }
    nc = bacc.Bacc("TRN2", target_bir_lowering=False, num_devices=1)
    given, args = {}, []
    for name in _INS:
        given[name] = np.ascontiguousarray(arrays[name])
        args.append(nc.dram_tensor(name, given[name].shape, mybir.dt.from_np(given[name].dtype), kind="ExternalInput").ap())
    out = nc.dram_tensor("out", (N, D), F32, kind="ExternalOutput").ap()
    gps_layer(nc, *args, out)
    r = run_bass_kernel_spmd(nc, [given], core_ids=[0])
    return r.results[0]["out"]
```
